# Optimizing a Trainium2 kernel written in Bass

```python
import numpy as np
import jax
import jax.numpy as jnp

def _softmax(x, axis=-1):
    return jax.nn.softmax(x, axis=axis)

def _gelu(x):
    return jax.nn.gelu(x, approximate=True)

def _silu(x):
    return jax.nn.silu(x)

def _sigmoid(x):
    return jax.nn.sigmoid(x)

def _layernorm(x, axis=-1, eps=1e-05):
    m = jnp.mean(x, axis=axis, keepdims=True)
    v = jnp.var(x, axis=axis, keepdims=True)
    return (x - m) / jnp.sqrt(v + eps)

def _scatter_add(tgt, idx, src, axis=0):
    return tgt.at[idx].add(src)

def _segment_sum(src, seg, n):
    return jax.ops.segment_sum(src, seg, n)
kernel_name = 'mk_prb_d1_jaxref_r8_f74e5c'

def setup_inputs(seed: int=0):
    np.random.seed(seed)
    _w = jnp.asarray

    def _L0_attn_setup():
        import jax, jax.numpy as jnp
        import numpy as np
        B, S, D = (2, 256, 128)
        H = 16
        K = 21
        HD = D // H

        def _tisa_bias(amplitudes, sharpness, offsets, seq_len):
            rel = jnp.arange(-(seq_len - 1), seq_len, dtype=jnp.float32)
            d = rel[None, None, :] - offsets[:, :, None]
            scores = amplitudes[:, :, None] * jnp.exp(-jnp.abs(sharpness)[:, :, None] * d * d)
            scores = scores.sum(axis=1)
            idx = jnp.arange(seq_len)
            rel_idx = idx[None, :] - idx[:, None] + (seq_len - 1)
            return scores[:, rel_idx]
        key = jax.random.key(seed)
        ks = jax.random.split(key, 7)
        x = jax.random.normal(ks[0], (B, S, D), dtype=jnp.float32)
        w_in = jax.random.normal(ks[1], (D, 3 * D), dtype=jnp.float32) * (1.0 / np.sqrt(D))
        w_gate = jax.random.normal(ks[2], (D, 2 * D), dtype=jnp.float32) * (1.0 / np.sqrt(D))
        b_gate = jnp.zeros((2 * D,), dtype=jnp.float32)
        amplitudes = jax.random.normal(ks[3], (H, K), dtype=jnp.float32) * 0.1
        sharpness = jax.random.uniform(ks[4], (H, K), dtype=jnp.float32, minval=0.05, maxval=0.3)
        max_fv, min_fv = (S // 2, 5)
        offsets = jax.random.uniform(ks[5], (H, K), dtype=jnp.float32, minval=-float(max_fv), maxval=float(max_fv))
        return {'x': x, 'w_in': w_in, 'w_gate': w_gate, 'b_gate': b_gate, 'amplitudes': amplitudes, 'sharpness': sharpness, 'offsets': offsets}
    _L0_attn_in = _L0_attn_setup()

    def _L0_ffn_setup():
        import jax, jax.numpy as jnp
        import numpy as np
        HIDDEN = 128
        INTER = 256
        NUM_EXPERTS = 8
        TOPK = 2
        STD = 0.02
        key = jax.random.key(seed)
        k1, k2, k3, k4 = jax.random.split(key, 4)
        return {'hidden_states': jax.random.normal(k1, (1, 256, HIDDEN), dtype=jnp.float32), 'w1': jax.random.normal(k2, (NUM_EXPERTS, 2 * INTER, HIDDEN), dtype=jnp.float32) * STD, 'w2': jax.random.normal(k3, (NUM_EXPERTS, HIDDEN, INTER), dtype=jnp.float32) * STD, 'router_w': jax.random.normal(k4, (NUM_EXPERTS, HIDDEN), dtype=jnp.float32) * STD}
    _L0_ffn_in = _L0_ffn_setup()
    _d = {'L0_attn_x': _L0_attn_in['x'], 'L0_attn_w_in': _L0_attn_in['w_in'], 'L0_attn_w_gate': _L0_attn_in['w_gate'], 'L0_attn_b_gate': _L0_attn_in['b_gate'], 'L0_attn_amplitudes': _L0_attn_in['amplitudes'], 'L0_attn_sharpness': _L0_attn_in['sharpness'], 'L0_attn_offsets': _L0_attn_in['offsets'], 'L0_ffn_w1': _L0_ffn_in['w1'], 'L0_ffn_w2': _L0_ffn_in['w2'], 'L0_ffn_router_w': _L0_ffn_in['router_w']}
    _x0 = _d['L0_attn_x']
    _d['L0_attn_x'] = jax.random.normal(jax.random.fold_in(jax.random.key(seed), 1), (4, 1024, 128), dtype=_x0.dtype)
    del _x0
    return _d

def reference(L0_attn_x, L0_attn_w_in, L0_attn_w_gate, L0_attn_b_gate, L0_attn_amplitudes, L0_attn_sharpness, L0_attn_offsets, L0_ffn_w1, L0_ffn_w2, L0_ffn_router_w):

    def _L0_attn_ref(x, w_in, w_gate, b_gate, amplitudes, sharpness, offsets):
        import jax, jax.numpy as jnp
        import numpy as np
        B, S, D = (2, 256, 128)
        H = 16
        K = 21
        HD = D // H

        def _tisa_bias(amplitudes, sharpness, offsets, seq_len):
            rel = jnp.arange(-(seq_len - 1), seq_len, dtype=jnp.float32)
            d = rel[None, None, :] - offsets[:, :, None]
            scores = amplitudes[:, :, None] * jnp.exp(-jnp.abs(sharpness)[:, :, None] * d * d)
            scores = scores.sum(axis=1)
            idx = jnp.arange(seq_len)
            rel_idx = idx[None, :] - idx[:, None] + (seq_len - 1)
            return scores[:, rel_idx]
        b, s, d = x.shape
        proj = x @ w_in
        k, v, q = jnp.split(proj, 3, axis=-1)

        def heads(t):
            return t.reshape(b, s, H, HD).transpose(0, 2, 1, 3)
        q, k, v = (heads(q), heads(k), heads(v))
        scale = 1.0 / jnp.sqrt(jnp.float32(HD))
        scores = jnp.einsum('bhqd,bhkd->bhqk', q, k) * scale
        scores = scores + _tisa_bias(amplitudes, sharpness, offsets, s)[None]
        weights = jax.nn.softmax(scores, axis=-1)
        attn = jnp.einsum('bhqk,bhkd->bhqd', weights, v)
        out = attn.transpose(0, 2, 1, 3).reshape(b, s, d)
        gated = out @ w_gate + b_gate
        a, g = jnp.split(gated, 2, axis=-1)
        return a * jax.nn.sigmoid(g)

    def _L0_ffn_ref(hidden_states, w1, w2, router_w):
        import jax, jax.numpy as jnp
        import numpy as np
        HIDDEN = 128
        INTER = 256
        NUM_EXPERTS = 8
        TOPK = 2
        STD = 0.02
        orig_shape = hidden_states.shape
        dtype = hidden_states.dtype
        x = hidden_states.reshape(-1, orig_shape[-1])
        E = w1.shape[0]
        gating = x @ router_w.T
        probs = jax.nn.softmax(gating.astype(jnp.float32), axis=-1)
        topk_w, sel = jax.lax.top_k(probs, TOPK)
        topk_w = topk_w.astype(dtype)
        combine = (jax.nn.one_hot(sel, E, dtype=dtype) * topk_w[..., None]).sum(axis=1)
        h = jnp.einsum('td,eid->tei', x, w1)
        gate = jax.nn.silu(h[..., :INTER])
        y = h[..., INTER:] * gate
        out = jnp.einsum('tei,ehi,te->th', y, w2, combine)
        return out.reshape(orig_shape)
    x = L0_attn_x
    xn = _layernorm(x, axis=-1)
    x = x + _L0_attn_ref(xn, L0_attn_w_in, L0_attn_w_gate, L0_attn_b_gate, L0_attn_amplitudes, L0_attn_sharpness, L0_attn_offsets) + _L0_ffn_ref(xn, L0_ffn_w1, L0_ffn_w2, L0_ffn_router_w)
    return x

_drawn_inputs = setup_inputs


def setup_inputs(seed=0):
    import zlib

    import numpy as np

    out = dict(_drawn_inputs(seed))
    spreads = {'L0_attn_b_gate': (0.0, 0.621)}
    factors = {'L0_attn_amplitudes': 175.052,
     'L0_attn_sharpness': 200.0,
     'L0_attn_offsets': 64.0,
     'L0_ffn_w1': 8.0,
     'L0_ffn_w2': 8.0,
     'L0_ffn_router_w': 8.0,
     'L0_attn_w_in': 4.019,
     'L0_attn_w_gate': 4.027}
    for name, (base, spread) in spreads.items():
        noise = np.random.default_rng([zlib.crc32(name.encode()), seed]).standard_normal(out[name].shape)
        drawn = base * np.exp(spread * noise) if base else spread * noise
        out[name] = jnp.asarray(drawn.astype(out[name].dtype))
    for name, factor in factors.items():
        out[name] = (out[name] * factor).astype(out[name].dtype)
    return out
```

```python
from contextlib import ExitStack

import concourse.bass as bass
from concourse import mybir

ALU = mybir.AluOpType
ACT = mybir.ActivationFunctionType
AX = mybir.AxisListType
F32 = mybir.dt.float32
BF16 = mybir.dt.bfloat16

P = 128


def fused_layer(nc, x, w_in, w_gate, b_gate, amplitudes, sharpness, offsets, w1, w2, router_w, out):
    B, S, D = x.shape
    H, K = amplitudes.shape
    HD = D // H
    E, I2, _ = w1.shape
    I = I2 // 2
    T = B * S // P
    G = T // 4
    ST = S // P
    NPART = 3
    KC = NPART * NPART * HD
    VC = 32
    OC = HD + 1
    REL = 2 * S
    RC = REL // P
    BW = S + (ST - 1) * P
    EPS = 1e-5
    SCALE = 1.0 / float(HD) ** 0.5
    LOWEST = -3.0e38
    UNITS = H * B
    TILES = UNITS * ST
    BODY = 2 * B * ST
    RING = 4
    SH_LAG = 2
    T_LAG, PV_LAG = 3, 11
    EV_LAG = PV_LAG + ST - 1
    OT_LAG = EV_LAG + 1

    qk_parts = nc.dram_tensor("qk_parts", (2, NPART, D, B * S), BF16).ap()
    qk_rows = nc.dram_tensor("qk_rows", (2, H, KC, B * S), BF16).ap()
    bias_dram = nc.dram_tensor("bias_rel", (H, REL), F32).ap()

    with ExitStack() as ctx:
        def sb(name, shape, dt=F32):
            return ctx.enter_context(nc.sbuf_tensor(name, shape, dt))

        def sem(name):
            return ctx.enter_context(nc.semaphore(name))

        ps = ctx.enter_context(nc.psum_tensor("ps", [P, 8, 512], F32))

        acc = sb("acc", [P, T, D])
        xnT = sb("xnT", [P, T * P])
        w1T = sb("w1T", [P, E, I2])
        w2T = sb("w2T", [P, E, 2, D])
        comb = sb("comb", [P, T, E])
        v_all = sb("v_all", [P, T, D])
        wi = sb("wi", [P, 3 * D])
        wg = sb("wg", [P, 2 * D])
        bg = sb("bg", [P, 2 * D])
        ident = sb("ident", [P, P])
        o_all = sb("o_all", [P, T, H, OC])
        pT = sb("pT", [P, 2, ST, S])
        shifted = sb("shifted", [P, RING, S])
        bias = sb("bias", [P, 2, BW])
        qs = sb("qs", [KC, 2, S], BF16)
        ks = sb("ks", [KC, 2, S], BF16)
        vu = sb("vu", [P, 2, ST, VC])
        rowmax = sb("rowmax", [P, 8])
        oT = sb("oT", [P, 2 * P])
        arena = pT[:, :, :, :].rearrange("p a b c -> p (a b c)")
        xn = arena[:, 0:T * P].rearrange("p (t d) -> p t d", d=D)
        w1n = arena[:, 4096:8192].rearrange("p (e j d) -> p e j d", e=E, d=D)
        w2n = arena[:, 8192:10240].rearrange("p (e i) -> p e i", e=E)
        bt = arena[:, 10240:10240 + RC * H * K].rearrange("p (c h k) -> p c h k", c=RC, h=H)
        ring = shifted[:, :, :].rearrange("p a b -> p (a b)")
        resid = ring[:, 0:1024].rearrange("p (a b) -> p a b", a=2)
        parts = ring[:, 1024:1024 + 1536].bitcast(BF16).rearrange("p (a n c) -> p a n c", a=2, n=NPART)
        par = ring[:, 2560:2560 + 3 * H * K].rearrange("p (n k) -> p n k", n=3)
        xrev = bias[:, 0, 0:1024].rearrange("p (a c) -> p a c", a=2)
        rel = sb("rel", [P, RC])
        flip = sb("flip", [P, P])
        bsum = sb("bsum", [P, RC, H])
        kept = o_all[:, :, :, :].rearrange("p a b c -> p (a b c)")
        bt2 = kept[:, 0:2 * P]
        stats = sb("stats", [P, T, 6])
        mv = sb("mv", [P, T, 2])
        std = sb("std", [P, T])
        rstd = sb("rstd", [P, T])
        eps = sb("eps", [P, 1])
        rtn = sb("rtn", [E, D])
        rT = sb("rT", [P, E])
        prio = sb("prio", [P, E])
        small = kept[:, 256:256 + 8 * T * E].rearrange("p (n t e) -> p n t e", n=8, t=T)
        sm1 = sb("sm1", [P, 6, T])
        gate_s = arena[:, 0:1024].rearrange("p (a b) -> p a b", a=2)
        y = arena[:, 1024:1024 + 2048].rearrange("p (a b c) -> p a b c", a=2, b=2)
        attn = arena[:, 0:4096].rearrange("p (t d) -> p t d", d=D)
        attnT = arena[:, 4096:8192]
        gated = arena[:, 8192:8192 + 2 * 512].rearrange("p (a t c) -> p a t c", a=2, t=2)
        sig = arena[:, 9216:9216 + 512].rearrange("p (a t c) -> p a t c", a=2, t=2)
        rsum = arena[:, 9728:9728 + T * H].rearrange("p (t h) -> p t h", t=T)

        x_tok = x.rearrange("b s d -> (b s) d").rearrange("(t p) d -> p t d", p=P)
        out_tok = out.rearrange("b s d -> (b s) d").rearrange("(t p) d -> p t d", p=P)

        XG = 4
        TG = T // XG
        s_x = [sem(f"x_loaded{i}") for i in range(XG)]
        s_win = sem("w_in_loaded")
        s_par = sem("bias_params_loaded")
        s_rt = sem("router_loaded")
        s_w1 = sem("w1_loaded")
        s_w2 = sem("w2_loaded")
        s_late = sem("gate_weights_loaded")
        s_eps = sem("eps_ready")
        s_id0 = sem("ident_zeroed")
        s_id = sem("ident_ready")
        s_fl = sem("flip_ready")
        s_xr = sem("xn_reversed")
        s_xrc = sem("xrev_copied")
        s_rel = sem("rel_ready")
        s_vz = sem("v_zeroed")
        s_stats = sem("stats_done")
        s_mv = sem("mean_var_done")
        s_std = sem("std_done")
        s_rstd = sem("rstd_done")
        s_xn = sem("xn_done")
        s_xt = sem("xn_transposed")
        s_xte = sem("xnT_copied")
        s_qk = sem("qk_projected")
        s_p1 = sem("part1_done")
        s_r1 = sem("rest1_done")
        s_p2 = sem("part2_done")
        s_p3 = sem("part3_done")
        s_pst = [sem(f"parts_stored{i}") for i in range(2)]
        s_fill = sem("wide_filled")
        s_cp = sem("wide_copied")
        s_rtT = sem("router_transposed")
        s_rtc = sem("router_copied")
        s_log = sem("logits_done")
        s_dv = sem("router_step")
        s_re = sem("router_exp")
        s_d = sem("bias_distance")
        s_bq = sem("bias_square")
        s_be = sem("bias_exp")
        s_ba = sem("bias_weighted")
        s_bs = sem("bias_summed")
        s_bT = sem("bias_transposed")
        s_bc = sem("bias_copied")
        s_bst = sem("bias_stored")

        def reversed_group(g):
            per = S // 512
            return g // per * per + per - 1 - g % per

        bt_flat = bt.rearrange("p c h k -> p c (h k)")
        with nc.Block() as block:
            @block.sync
            def _(sp):
                for i in range(XG):
                    sp.dma_start(acc[:, i * TG:(i + 1) * TG, :], x_tok[:, i * TG:(i + 1) * TG, :]).then_inc(s_x[i], 16)
                    if i == 0:
                        sp.dma_start(wi[:, :], w_in).then_inc(s_win, 16)
                for n, a in enumerate((amplitudes, sharpness, offsets)):
                    sp.dma_start(par[:, n, :], a.rearrange("h k -> (h k)").partition_broadcast(P)).then_inc(s_par, 16)
                sp.dma_start(rtn[:, :], router_w).then_inc(s_rt, 16)
                sp.dma_start(w1n, w1.rearrange("e (j p) d -> p e j d", p=P)).then_inc(s_w1, 16)
                sp.dma_start(w2n, w2.rearrange("e h i -> h e i")).then_inc(s_w2, 16)
                sp.dma_start(wg[:, :], w_gate).then_inc(s_late, 16)
                sp.dma_start(bg[:, :], b_gate.partition_broadcast(P)).then_inc(s_late, 16)
                for j in range(2 * G):
                    g, w = j // 2, j % 2
                    if w:
                        g = reversed_group(g)
                    sp.wait_ge(s_p3, j + 1)
                    sp.wait_ge(s_p2, j + 1)
                    sp.dma_start(qk_parts[w, :, :, g * 512:(g + 1) * 512].rearrange("n d t -> d n t"),
                                 parts[:, j % 2, :, :]).then_inc(s_pst[j % 2], 16)
                sp.wait_ge(s_bc, 1)
                for n in range(2):
                    sp.dma_start(bias_dram.rearrange("h (c r) -> c h r", r=P)[8 * n:8 * n + 8],
                                 bt2[:, n * P:(n + 1) * P]).then_inc(s_bst, 16)
                for a in s_pst:
                    sp.wait_ge(a, 16 * G)
                sp.wait_ge(s_bst, 32)
                sp.wait_ge(s_late, 32)

            @block.gpsimd
            def _(pool):
                nc.gpsimd.memset(eps[:, :], EPS).then_inc(s_eps, 1)
                nc.gpsimd.memset(ident[:, :], 0.0).then_inc(s_id0, 1)
                pool.wait_ge(s_id0, 1)
                nc.gpsimd.affine_select(out=ident[:, :], in_=ident[:, :], compare_op=ALU.not_equal, fill=1.0,
                                        base=0, pattern=[[-1, P]], channel_multiplier=1).then_inc(s_id, 1)
                nc.gpsimd.memset(flip[:, :], 0.0).then_inc(s_fl, 1)
                pool.wait_ge(s_fl, 1)
                nc.gpsimd.affine_select(out=flip[:, :], in_=flip[:, :], compare_op=ALU.not_equal, fill=1.0,
                                        base=-(P - 1), pattern=[[1, P]], channel_multiplier=1).then_inc(s_fl, 1)
                nc.gpsimd.iota(rel[:, :], pattern=[[-P, RC]], base=S - 1, channel_multiplier=-1,
                               allow_small_or_imprecise_dtypes=True).then_inc(s_rel, 1)
                nc.gpsimd.iota(prio[:, :], pattern=[[-1, E]], base=E, channel_multiplier=0,
                               allow_small_or_imprecise_dtypes=True).then_inc(s_rel, 1)
                nc.gpsimd.memset(vu[:, :, :, :], 0.0).then_inc(s_vz, 1)
                pool.wait_ge(s_vz, 1)
                nc.gpsimd.memset(vu[:, :, :, HD:HD + 1], 1.0).then_inc(s_vz, 1)
                for c in range(RC):
                    pool.wait_ge(s_d, c + 2)
                    nc.gpsimd.tensor_tensor(bt_flat[:, c, :], bt_flat[:, c, :], bt_flat[:, c, :],
                                            ALU.mult).then_inc(s_bq, 1)
                for c in range(RC):
                    pool.wait_ge(s_bq, c + 1)
                    nc.gpsimd.tensor_tensor(bt_flat[:, c, :], bt_flat[:, c, :], par[:, 1, :],
                                            ALU.mult).then_inc(s_bq, 1)
                for c in range(RC):
                    pool.wait_ge(s_be, c + 1)
                    nc.gpsimd.tensor_tensor(bt_flat[:, c, :], bt_flat[:, c, :], par[:, 0, :],
                                            ALU.mult).then_inc(s_ba, 1)

            @block.vector
            def _(dve):
                def statistics(i):
                    dve.wait_ge(s_x[i], 16)
                    for t in range(i * TG, (i + 1) * TG):
                        nc.vector.bn_stats(stats[:, t, :], acc[:, t, :]).then_inc(s_stats, 1)
                    for t in range(i * TG, (i + 1) * TG):
                        dve.wait_ge(s_stats, t + 1)
                        nc.vector.bn_aggr(mv[:, t, :], stats[:, t, :]).then_inc(s_mv, 1)

                def normalise(i):
                    dve.wait_ge(s_std, i + 1)
                    nc.vector.reciprocal(rstd[:, i * TG:(i + 1) * TG], std[:, i * TG:(i + 1) * TG]).then_inc(s_rstd, 1)
                    dve.wait_ge(s_rstd, i + 1)
                    for t in range(i * TG, (i + 1) * TG):
                        nc.vector.tensor_scalar(xn[:, t, :], acc[:, t, :], mv[:, t, 0:1], rstd[:, t:t + 1],
                                                ALU.subtract, ALU.mult).then_inc(s_xn, 1)

                statistics(0)
                for i in range(XG):
                    if i + 1 < XG:
                        statistics(i + 1)
                    normalise(i)

                dve.wait_ge(s_par, 48)
                dve.wait_ge(s_rel, 2)
                nc.vector.scalar_tensor_tensor(out=par[:, 1, :], in0=par[:, 1, :], scalar=-1.0, in1=par[:, 1, :],
                                               op0=ALU.mult, op1=ALU.max).then_inc(s_d, 1)
                for c in range(RC):
                    nc.vector.tensor_scalar(bt_flat[:, c, :], par[:, 2, :], rel[:, c:c + 1], None,
                                            ALU.subtract).then_inc(s_d, 1)

                def first_rest(j):
                    dve.wait_ge(s_p1, j + 1)
                    if j >= 2:
                        dve.wait_ge(s_p3, j - 1)
                    sc = SCALE if j % 2 == 0 else 1.0
                    nc.vector.scalar_tensor_tensor(out=resid[:, j % 2, :], in0=ps[:, 2 + j % 2, :], scalar=sc,
                                                   in1=parts[:, j % 2, 0, :], op0=ALU.mult,
                                                   op1=ALU.subtract).then_inc(s_r1, 1)

                def last_part(j):
                    dve.wait_ge(s_p2, j + 1)
                    nc.vector.tensor_tensor(parts[:, j % 2, 2, :], resid[:, j % 2, :], parts[:, j % 2, 1, :],
                                            ALU.subtract).then_inc(s_p3, 1)

                dve.wait_ge(s_rtT, 1)
                nc.vector.tensor_copy(rT[:, :], ps[:, 6, 0:E]).then_inc(s_rtc, 1)
                for j in range(2 * G + 1):
                    if j < 2 * G:
                        first_rest(j)
                    if j >= 1:
                        last_part(j - 1)

                logits = ps[:, 6, 0:T * E].rearrange("p (t e) -> p t e", e=E)
                lg, pr, eq, sel1, rest, eq2, sel2 = (small[:, n] for n in range(7))
                mx, sm, rs, top, mxr, top2 = (sm1[:, n] for n in range(6))

                def bc(a):
                    return a.unsqueeze(2).to_broadcast([P, T, E])

                done = [0]

                def step(ins):
                    done[0] += 1
                    ins.then_inc(s_dv, 1)
                    dve.wait_ge(s_dv, done[0])

                pri = prio[:, :].unsqueeze(1).to_broadcast([P, T, E])
                dve.wait_ge(s_log, 1)
                step(nc.vector.tensor_reduce(mx, logits, AX.X, ALU.max))
                step(nc.vector.tensor_tensor(lg, logits, bc(mx), ALU.subtract))
                dve.wait_ge(s_re, 1)
                step(nc.vector.tensor_reduce(sm, pr, AX.X, ALU.add))
                step(nc.vector.reciprocal(rs, sm))
                step(nc.vector.tensor_tensor(pr, pr, bc(rs), ALU.mult))
                step(nc.vector.tensor_reduce(mx, pr, AX.X, ALU.max))
                step(nc.vector.tensor_tensor(eq, pr, bc(mx), ALU.is_equal))
                step(nc.vector.tensor_tensor(eq, eq, pri, ALU.mult))
                step(nc.vector.tensor_reduce(top, eq, AX.X, ALU.max))
                step(nc.vector.tensor_tensor(sel1, eq, bc(top), ALU.is_equal))
                step(nc.vector.scalar_tensor_tensor(out=rest, in0=sel1, scalar=-2.0, in1=pr, op0=ALU.mult, op1=ALU.add))
                step(nc.vector.tensor_reduce(mxr, rest, AX.X, ALU.max))
                step(nc.vector.tensor_tensor(eq2, rest, bc(mxr), ALU.is_equal))
                step(nc.vector.tensor_tensor(eq2, eq2, pri, ALU.mult))
                step(nc.vector.tensor_reduce(top2, eq2, AX.X, ALU.max))
                step(nc.vector.tensor_tensor(sel2, eq2, bc(top2), ALU.is_equal))
                step(nc.vector.tensor_tensor(sel1, sel1, sel2, ALU.add))
                step(nc.vector.tensor_tensor(comb[:, :, :], sel1, pr, ALU.mult))

                dve.wait_ge(s_ba, RC)
                nc.vector.tensor_reduce(bsum[:, :, :], bt, AX.X, ALU.add).then_inc(s_bs, 1)
                dve.wait_ge(s_bT, 1)
                nc.vector.tensor_copy(bt2[:, :], ps[:, 7, 0:256]).then_inc(s_bc, 1)

            @block.scalar
            def _(act):
                for i in range(XG):
                    act.wait_ge(s_mv, (i + 1) * TG)
                    act.wait_ge(s_eps, 1)
                    nc.scalar.activation(std[:, i * TG:(i + 1) * TG], mv[:, i * TG:(i + 1) * TG, 1], ACT.Sqrt,
                                         bias=eps[:, 0:1], scale=1.0).then_inc(s_std, 1)

                def xnT_copy(g):
                    act.wait_ge(s_xt, g + 1)
                    nc.scalar.copy(xnT[:, g * 512:(g + 1) * 512], ps[:, g % 2, :]).then_inc(s_xte, 1)

                def xrev_copy(g):
                    act.wait_ge(s_xr, g + 1)
                    if g >= 2:
                        act.wait_ge(s_qk, 2 * g - 2)
                        act.wait_ge(s_fill, g - 1)
                    nc.scalar.copy(xrev[:, g % 2, :], ps[:, 7, :]).then_inc(s_xrc, 1)

                def first_part(j):
                    act.wait_ge(s_qk, j + 1)
                    if j >= 2:
                        act.wait_ge(s_pst[j % 2], 16 * (j // 2))
                    sc = SCALE if j % 2 == 0 else 1.0
                    nc.scalar.mul(parts[:, j % 2, 0, :], ps[:, 2 + j % 2, :], sc).then_inc(s_p1, 1)

                def second_part(j):
                    act.wait_ge(s_r1, j + 1)
                    nc.scalar.copy(parts[:, j % 2, 1, :], resid[:, j % 2, :]).then_inc(s_p2, 1)

                def wide_copy(n):
                    act.wait_ge(s_fill, n + 1)
                    src = ps[:, 4 + n % 2, :]
                    if n < G:
                        k = 4 * reversed_group(n)
                        nc.scalar.copy(v_all[:, k:k + 4, :].rearrange("p t d -> p (t d)"), src).then_inc(s_cp, 1)
                    elif n < G + E:
                        nc.scalar.copy(w1T[:, n - G, :], src).then_inc(s_cp, 1)
                    else:
                        m = n - G - E
                        nc.scalar.copy(w2T[:, 2 * m:2 * m + 2, :, :].rearrange("p e i d -> p (e i d)"),
                                       src).then_inc(s_cp, 1)

                xnT_copy(0)
                xrev_copy(0)
                for g in range(G):
                    if g + 1 < G:
                        xnT_copy(g + 1)
                        xrev_copy(g + 1)
                    first_part(2 * g)
                    if g:
                        second_part(2 * g - 1)
                    first_part(2 * g + 1)
                    second_part(2 * g)
                    wide_copy(g)
                second_part(2 * G - 1)
                for n in range(G, G + E + E // 2):
                    wide_copy(n)
                act.wait_ge(s_dv, 2)
                nc.scalar.activation(small[:, 1], small[:, 0], ACT.Exp).then_inc(s_re, 1)
                for c in range(RC):
                    act.wait_ge(s_bq, RC + c + 1)
                    nc.scalar.activation(bt_flat[:, c, :], bt_flat[:, c, :], ACT.Exp, scale=-1.0).then_inc(s_be, 1)

            @block.tensor
            def _(pe):
                pe.wait_ge(s_id, 1)
                pe.wait_ge(s_rt, 16)
                nc.tensor.transpose(ps[:, 6, 0:E], rtn[:, :], ident[0:E, 0:E]).then_inc(s_rtT, 1)

                def turn_xn(g):
                    pe.wait_ge(s_xn, 4 * g + 4)
                    if g >= 2:
                        pe.wait_ge(s_xte, g - 1)
                    for t in range(4):
                        mm = nc.tensor.transpose(ps[:, g % 2, t * P:(t + 1) * P], xn[:, 4 * g + t, :], ident[:, :])
                    mm.then_inc(s_xt, 1)

                def turn_reversed(g):
                    if g >= 1:
                        pe.wait_ge(s_xrc, g)
                    pe.wait_ge(s_xn, 4 * g + 4)
                    for t in range(4):
                        mm = nc.tensor.transpose(ps[:, 7, (3 - t) * P:(4 - t) * P], xn[:, 4 * g + t, :], flip[:, :])
                    mm.then_inc(s_xr, 1)

                def project(j):
                    g, w = j // 2, j % 2
                    pe.wait_ge(s_xrc if w else s_xte, g + 1)
                    if j >= 2:
                        pe.wait_ge(s_p1, j - 1)
                        pe.wait_ge(s_r1, j - 1)
                    col = 2 * D if w == 0 else 0
                    tokens = xrev[:, g % 2, :] if w else xnT[:, g * 512:(g + 1) * 512]
                    nc.tensor.matmul(ps[:, 2 + j % 2, :], wi[:, col:col + D], tokens,
                                     start=True, stop=True).then_inc(s_qk, 1)

                def wide(n):
                    if n >= 2:
                        pe.wait_ge(s_cp, n - 1)
                    for t in range(4):
                        dst = ps[:, 4 + n % 2, t * P:(t + 1) * P]
                        if n < G:
                            mm = nc.tensor.matmul(dst, xrev[:, n % 2, t * P:(t + 1) * P], wi[:, D:2 * D],
                                                  start=True, stop=True)
                        elif n < G + E:
                            mm = nc.tensor.transpose(dst, w1n[:, n - G, t, :], ident[:, :])
                        else:
                            e, i = 2 * (n - G - E) + t // 2, t % 2
                            mm = nc.tensor.transpose(dst, w2n[:, e, i * P:(i + 1) * P], ident[:, :])
                    mm.then_inc(s_fill, 1)

                turn_xn(0)
                pe.wait_ge(s_fl, 2)
                turn_reversed(0)
                pe.wait_ge(s_win, 16)
                for g in range(G):
                    if g + 1 < G:
                        turn_xn(g + 1)
                        turn_reversed(g + 1)
                    project(2 * g)
                    project(2 * g + 1)
                    wide(g)
                pe.wait_ge(s_w1, 16)
                pe.wait_ge(s_rtc, 1)
                for t in range(T):
                    mm = nc.tensor.matmul(ps[:, 6, t * E:(t + 1) * E], xnT[:, t * P:(t + 1) * P], rT[:, :],
                                          start=True, stop=True)
                mm.then_inc(s_log, 1)
                for n in range(G, G + E):
                    wide(n)
                pe.wait_ge(s_w2, 16)
                for n in range(G + E, G + E + E // 2):
                    wide(n)
                pe.wait_ge(s_bs, 1)
                pe.wait_ge(s_xrc, G)
                bflat = bsum[:, :, :].rearrange("p c h -> p (c h)")
                for n in range(2):
                    mm = nc.tensor.transpose(ps[:, 7, n * P:(n + 1) * P], bflat[:, n * P:(n + 1) * P], ident[:, :])
                mm.then_inc(s_bT, 1)

        def wait(eng, s, it, per, n):
            if isinstance(it, int):
                n, it = n + it * per, None
                if n <= 0:
                    return
            eng.wait_ge(s, n if it is None else it * per + n)

        def sweep(eng, times, body, lag, first, step):
            for k in range(first):
                step(0, k)
            with eng.Fori(0, times - 1) as it:
                for k in range(first, first + body):
                    step(it, k)
            for k in range(first, body + lag):
                step(times - 1, k)

        s_gu = sem("gate_up_done")
        s_sg = sem("silu_done")
        s_y = sem("y_done")
        s_dn = sem("down_done")
        s_ac = sem("expert_added")
        s_row = sem("rows_stacked")
        with nc.Block() as block:
            @block.sync
            def _(sp):
                stacked = qk_rows.rearrange("w h (n m d) t -> w n m h d t", n=NPART, m=NPART)
                for n in range(NPART):
                    for m in range(NPART):
                        for w in range(2):
                            src = qk_parts[w, m if w else n].rearrange("(h d) t -> h d t", d=HD)
                            sp.dma_start(stacked[w, n, m], src).then_inc(s_row, 16)
                sp.wait_ge(s_row, 16 * 2 * NPART * NPART)

            def tiles(it, k, s):
                n = (it + k // E) * 4 + s
                return slice(n, n + 1) if isinstance(it, int) else bass.ds(n, 1)

            def block_of(it, k):
                n = (it + k // E) * 512
                return slice(n, n + 512) if isinstance(it, int) else bass.ds(n, 512)

            def runs(it, k):
                return k >= 0 and (not isinstance(it, int) or it * E + k < G * E)

            @block.tensor
            def _(pe):
                def gate_up(it, k):
                    e = k % E
                    for half in range(2):
                        n = 2 * k + half
                        wait(pe, s_y, it, 2 * E, n - 1)
                        for u in range(2):
                            col = u * I + half * P
                            nc.tensor.matmul(ps[:, 2 * half + u, :], w1T[:, e, col:col + P],
                                             xnT[:, block_of(it, k)], start=True, stop=True).then_inc(s_gu, 1)

                def down(it, k):
                    wait(pe, s_y, it, 2 * E, 2 * k + 2)
                    wait(pe, s_ac, it, 4 * E, 4 * (k - 1))
                    for s in range(4):
                        for half in range(2):
                            mm = nc.tensor.matmul(ps[:, 4 + k % 2, s * P:(s + 1) * P],
                                                  y[:, k % 2, half, s * P:(s + 1) * P], w2T[:, k % E, half, :],
                                                  start=(half == 0), stop=(half == 1))
                    mm.then_inc(s_dn, 1)

                def step(it, k):
                    if runs(it, k):
                        gate_up(it, k)
                    if runs(it, k - 1):
                        down(it, k - 1)

                sweep(pe, G, E, 1, 3, step)

            @block.scalar
            def _(act):
                def step(it, k):
                    for half in range(2):
                        n = 2 * k + half
                        wait(act, s_gu, it, 4 * E, 2 * n + 1)
                        wait(act, s_y, it, 2 * E, n - 1)
                        nc.scalar.activation(gate_s[:, half, :], ps[:, 2 * half, :], ACT.Silu).then_inc(s_sg, 1)

                sweep(act, G, E, 0, 2, step)

            @block.vector
            def _(dve):
                def multiply(it, k):
                    for half in range(2):
                        n = 2 * k + half
                        wait(dve, s_sg, it, 2 * E, n + 1)
                        wait(dve, s_gu, it, 4 * E, 2 * n + 2)
                        wait(dve, s_dn, it, E, k - 1)
                        nc.vector.tensor_tensor(y[:, k % 2, half, :], ps[:, 2 * half + 1, :], gate_s[:, half, :],
                                                ALU.mult).then_inc(s_y, 1)

                def add(it, k):
                    wait(dve, s_dn, it, E, k + 1)
                    for s in range(4):
                        wait(dve, s_ac, it, 4 * E, 4 * (k - 1) + s + 1)
                        a = acc[:, tiles(it, k, s), :].rearrange("p a d -> p (a d)")
                        w = comb[:, tiles(it, k, s), k % E:k % E + 1].rearrange("p a d -> p (a d)")
                        nc.vector.scalar_tensor_tensor(out=a, in0=ps[:, 4 + k % 2, s * P:(s + 1) * P], scalar=w,
                                                       in1=a, op0=ALU.mult, op1=ALU.add).then_inc(s_ac, 1)

                def step(it, k):
                    if runs(it, k):
                        multiply(it, k)
                    if runs(it, k - 1):
                        add(it, k - 1)

                sweep(dve, G, E, 1, 3, step)

        s_ql = [sem(f"qk_loaded{i}") for i in range(2)]
        s_bl = [sem(f"bias_loaded{i}") for i in range(2)]
        s_vc = sem("v_copied")
        s_s = sem("scores_done")
        s_m = sem("max_done")
        s_sh = sem("shift_done")
        s_tr = sem("half_transposed")
        s_e = sem("half_exped")
        s_pv = sem("pv_piece_done")
        s_ev = sem("out_copied")
        s_ot = sem("out_transposed")
        s_oc = sem("out_kept")
        o_tiles = o_all[:, :, :, :].rearrange("p (b j s) h c -> p s b j h c", b=B, j=4, s=2)

        def within(it, k):
            return k >= 0 and (not isinstance(it, int) or it * BODY + k < TILES)

        LOADS = 2
        U = BODY // ST
        with nc.Block() as block:
            @block.sync
            def _(sp):
                def load_unit(it, u):
                    wait(sp, s_s, it, BODY, ST * (u - 1))
                    h = it * 2 + u // B
                    b = u % B
                    col = slice(b * S, (b + 1) * S)
                    for w, dst in enumerate((qs, ks)):
                        src = qk_rows[w, h, :, col] if isinstance(it, int) else \
                            qk_rows[w, bass.ds(h, 1), :, col].rearrange("a r t -> (a r) t")
                        sp.dma_start(dst[:, u % 2, :], src).then_inc(s_ql[u % 2], 16)

                def load_bias(it, hh):
                    wait(sp, s_m, it, BODY, B * ST * (hh - 1))
                    h = it * 2 + hh
                    row = bias_dram[h, :] if isinstance(it, int) else bias_dram[bass.ds(h, 1), :]
                    src = bass.AP(row.tensor, row.offset, [[1, P], [1, BW]])
                    sp.dma_start(bias[:, hh % 2, :], src).then_inc(s_bl[hh % 2], 16)

                load_bias(0, 0)
                load_unit(0, 0)
                load_unit(0, 1)
                load_bias(0, 1)
                with sp.Fori(0, TILES // BODY - 1) as it:
                    for u in range(2, U + 2):
                        load_unit(it, u)
                        if u == B + 1:
                            load_bias(it, 2)
                    load_bias(it, 3)
                for u in range(2, U):
                    load_unit(TILES // BODY - 1, u)

            @block.gpsimd
            def _(pool):
                def copy_v(it, u):
                    wait(pool, s_pv, it, BODY, ST * (u - 1))
                    h = it * 2 + u // B
                    b = u % B
                    cols = slice(h * HD, (h + 1) * HD) if isinstance(it, int) else bass.ds(h * HD, HD)
                    nc.gpsimd.tensor_copy(vu[:, u % 2, :, 0:HD], v_all[:, b * ST:(b + 1) * ST, cols]).then_inc(s_vc, 1)

                copy_v(0, 0)
                copy_v(0, 1)
                with pool.Fori(0, TILES // BODY - 1) as it:
                    for u in range(2, U + 2):
                        copy_v(it, u)
                for u in range(2, U):
                    copy_v(TILES // BODY - 1, u)

            @block.tensor
            def _(pe):
                def scores(it, k):
                    u = k // ST
                    if k % ST == 0:
                        wait(pe, s_ql[u % 2], it, 16 * LOADS * U // 2, 16 * LOADS * (u // 2 + 1))
                    wait(pe, s_m, it, BODY, k - 1)
                    for n in range(2):
                        mm = nc.tensor.matmul(ps[:, 2 * (k % 2) + n, :], qs[:, u % 2, (k % ST) * P:(k % ST + 1) * P],
                                              ks[:, u % 2, n * 512:(n + 1) * 512], start=True, stop=True)
                    mm.then_inc(s_s, 1)

                def turn(it, k, half):
                    if half == 0:
                        wait(pe, s_sh, it, BODY, k + 1)
                    wait(pe, s_e, it, 2 * BODY, 2 * k + half - 1)
                    for c in range(4):
                        col = (4 * half + c) * P
                        mm = nc.tensor.transpose(ps[:, 4 + half, c * P:(c + 1) * P],
                                                 shifted[:, k % RING, col:col + P], ident[:, :])
                    mm.then_inc(s_tr, 1)

                def weigh(it, k):
                    u, kt = k // ST, k % ST
                    if kt == 0:
                        wait(pe, s_e, it, 2 * BODY, 2 * ST * (u + 1))
                        wait(pe, s_vc, it, U, u + 1)
                        wait(pe, s_ev, it, U, u)
                    for j in range(4):
                        mm = nc.tensor.matmul(ps[32 * j:32 * j + 32, 6, 0:256], vu[:, u % 2, kt, :],
                                              pT[:, u % 2, kt, j * 256:(j + 1) * 256],
                                              start=(kt == 0), stop=(kt == ST - 1), tile_position=(0, 32 * j))
                    mm.then_inc(s_pv, 1)

                def turn_out(it, u):
                    wait(pe, s_ev, it, U, u + 1)
                    wait(pe, s_oc, it, U, u)
                    for s in range(2):
                        mm = nc.tensor.transpose(ps[:, 7, s * P:(s + 1) * P], oT[:, s * P:(s + 1) * P], ident[:, :])
                    mm.then_inc(s_ot, 1)

                def step(it, k):
                    if within(it, k):
                        scores(it, k)
                    if within(it, k - T_LAG):
                        turn(it, k - T_LAG, 0)
                    if within(it, k - PV_LAG):
                        weigh(it, k - PV_LAG)
                    if within(it, k - T_LAG):
                        turn(it, k - T_LAG, 1)
                    if k >= OT_LAG and (k - OT_LAG) % ST == 0:
                        turn_out(it, (k - OT_LAG) // ST)

                sweep(pe, TILES // BODY, BODY, PV_LAG + 1, OT_LAG + 1, step)

            @block.vector
            def _(dve):
                def may_add(it, k):
                    if k % (B * ST) == 0:
                        hh = k // (B * ST)
                        wait(dve, s_bl[hh % 2], it, 16, 16 * (hh // 2 + 1))
                    wait(dve, s_s, it, BODY, k + 1)
                    wait(dve, s_tr, it, 2 * BODY, 2 * (k - RING) + 2)
                    wait(dve, s_sh, it, BODY, k - RING + 1)

                def add_max(it, k):
                    off = (k % ST) * P
                    nc.vector.tensor_tensor_reduce(
                        shifted[:, k % RING, :],
                        ps[:, 2 * (k % 2):2 * (k % 2) + 2, :].rearrange("p a b -> p (a b)"),
                        bias[:, (k // (B * ST)) % 2, off:off + S], 1.0, LOWEST, ALU.add, ALU.max,
                        rowmax[:, k % 8:k % 8 + 1]).then_inc(s_m, 1)

                def shift(it, k):
                    wait(dve, s_m, it, BODY, k + 1)
                    nc.vector.tensor_scalar(shifted[:, k % RING, :], shifted[:, k % RING, :],
                                            rowmax[:, k % 8:k % 8 + 1], None, ALU.subtract).then_inc(s_sh, 1)

                def step(it, k):
                    if within(it, k):
                        may_add(it, k)
                    if within(it, k - SH_LAG):
                        shift(it, k - SH_LAG)
                    if within(it, k):
                        add_max(it, k)

                sweep(dve, TILES // BODY, BODY, SH_LAG, ST, step)

            @block.scalar
            def _(act):
                def expo(it, k, half):
                    u = k // ST
                    wait(act, s_tr, it, 2 * BODY, 2 * k + half + 1)
                    if k % ST == 0:
                        wait(act, s_pv, it, BODY, ST * (u - 1))
                    q = (k % ST) * P
                    nc.scalar.activation(pT[:, u % 2, 4 * half:4 * half + 4, q:q + P],
                                         ps[:, 4 + half, :].rearrange("p (a b) -> p a b", a=4),
                                         ACT.Exp).then_inc(s_e, 1)

                def keep_sum(it, u):
                    wait(act, s_pv, it, BODY, ST * (u + 1))
                    wait(act, s_ot, it, U, u)
                    nc.scalar.copy(oT[:, :], ps[:, 6, 0:256]).then_inc(s_ev, 1)

                def keep_out(it, u):
                    wait(act, s_ot, it, U, u + 1)
                    b = u % B
                    h = it * 2 + u // B
                    for s in range(2):
                        src = ps[:, 7, s * P:(s + 1) * P].rearrange("p (j c) -> p j c", j=4)[:, :, 0:OC]
                        if isinstance(it, int):
                            dst = o_tiles[:, s, b, :, h, :]
                        else:
                            dst = o_tiles[:, s, b, :, bass.ds(h, 1), :].rearrange("p j a c -> p j (a c)")
                        ins = nc.scalar.copy(dst, src)
                    ins.then_inc(s_oc, 1)

                def step(it, k):
                    if within(it, k - T_LAG):
                        expo(it, k - T_LAG, 0)
                        expo(it, k - T_LAG, 1)
                    if k >= EV_LAG and (k - EV_LAG) % ST == 0:
                        keep_sum(it, (k - EV_LAG) // ST)
                    if k >= OT_LAG and (k - OT_LAG) % ST == 0:
                        keep_out(it, (k - OT_LAG) // ST)

                sweep(act, TILES // BODY, BODY, PV_LAG + 1, OT_LAG, step)

        s_rc = sem("sums_inverted")
        s_an = sem("attn_normalised")
        s_at = sem("attn_transposed")
        s_atc = sem("attnT_copied")
        s_gt = sem("gate_projected")
        s_gb = sem("gate_biased")
        s_si = sem("sigmoid_done")
        s_ml = sem("gated_done")
        s_fi = sem("result_done")
        s_out = sem("result_stored")
        NP2 = T // 2
        with nc.Block() as block:
            @block.vector
            def _(dve):
                nc.vector.reciprocal(rsum, o_all[:, :, :, HD]).then_inc(s_rc, 1)
                dve.wait_ge(s_rc, 1)

                def norm(g):
                    t = slice(4 * g, 4 * g + 4)
                    nc.vector.tensor_tensor(attn[:, t, :].rearrange("p t (h c) -> p (t h) c", c=HD),
                                            o_all[:, t, :, 0:HD].rearrange("p t h c -> p (t h) c"),
                                            rsum[:, t, :].rearrange("p t h -> p (t h)").unsqueeze(2)
                                            .to_broadcast([P, 4 * H, HD]), ALU.mult).then_inc(s_an, 1)

                def biased(n):
                    dve.wait_ge(s_gt, n + 1)
                    if n >= 2:
                        dve.wait_ge(s_ml, n - 1)
                    nc.vector.tensor_tensor(gated[:, n % 2], ps[:, 4 + n % 2, :].rearrange("p (t c) -> p t c", t=2),
                                            bg[:, :].unsqueeze(1).to_broadcast([P, 2, 2 * D]),
                                            ALU.add).then_inc(s_gb, 1)

                def final(n):
                    dve.wait_ge(s_si, n + 1)
                    nc.vector.tensor_tensor(sig[:, n % 2], gated[:, n % 2, :, 0:D], sig[:, n % 2],
                                            ALU.mult).then_inc(s_ml, 1)
                    dve.wait_ge(s_ml, n + 1)
                    a = acc[:, 2 * n:2 * n + 2, :]
                    nc.vector.tensor_tensor(a, a, sig[:, n % 2], ALU.add).then_inc(s_fi, 1)

                norm(0)
                norm(1)
                for n in range(NP2 + 1):
                    if n % 2 == 0 and n // 2 + 2 < G:
                        norm(n // 2 + 2)
                    if n < NP2:
                        biased(n)
                    if n:
                        final(n - 1)

            @block.scalar
            def _(act):
                def copy_t(g):
                    act.wait_ge(s_at, g + 1)
                    nc.scalar.copy(attnT[:, g * 512:(g + 1) * 512], ps[:, g % 2, :]).then_inc(s_atc, 1)

                copy_t(0)
                for n in range(NP2):
                    if n % 2 == 0 and n // 2 + 1 < G:
                        copy_t(n // 2 + 1)
                    act.wait_ge(s_gb, n + 1)
                    if n >= 2:
                        act.wait_ge(s_fi, n - 1)
                    nc.scalar.activation(sig[:, n % 2], gated[:, n % 2, :, D:2 * D], ACT.Sigmoid).then_inc(s_si, 1)

            @block.tensor
            def _(pe):
                def turn_attn(g):
                    pe.wait_ge(s_an, g + 1)
                    if g >= 2:
                        pe.wait_ge(s_atc, g - 1)
                    for t in range(4):
                        mm = nc.tensor.transpose(ps[:, g % 2, t * P:(t + 1) * P], attn[:, 4 * g + t, :], ident[:, :])
                    mm.then_inc(s_at, 1)

                turn_attn(0)
                for n in range(NP2):
                    if n % 2 == 0:
                        if n // 2 + 1 < G:
                            turn_attn(n // 2 + 1)
                        pe.wait_ge(s_atc, n // 2 + 1)
                    if n >= 2:
                        pe.wait_ge(s_gb, n - 1)
                    for t in range(2):
                        k = 2 * n + t
                        mm = nc.tensor.matmul(ps[:, 4 + n % 2, t * 2 * D:(t + 1) * 2 * D],
                                              attnT[:, k * P:(k + 1) * P], wg[:, :], start=True, stop=True)
                    mm.then_inc(s_gt, 1)

            @block.sync
            def _(sp):
                for g in range(G):
                    sp.wait_ge(s_fi, 2 * g + 2)
                    sp.dma_start(out_tok[:, 4 * g:4 * g + 4, :], acc[:, 4 * g:4 * g + 4, :]).then_inc(s_out, 16)
                sp.wait_ge(s_out, 16 * G)


_INS = ['L0_attn_x', 'L0_attn_w_in', 'L0_attn_w_gate', 'L0_attn_b_gate', 'L0_attn_amplitudes', 'L0_attn_sharpness',
        'L0_attn_offsets', 'L0_ffn_w1', 'L0_ffn_w2', 'L0_ffn_router_w']
_OUTS = [((4, 1024, 128), 'float32')]


def kernel(**inputs):
    import numpy as _np
    import concourse.bacc as _bacc
    from concourse import mybir as _mybir
    from concourse.bass_utils import run_bass_kernel_spmd as _run

    nc = _bacc.Bacc("TRN2", target_bir_lowering=False, num_devices=1)
    arrays, args = {}, []
    for name in _INS:
        a = _np.ascontiguousarray(inputs[name])
        arrays[f"in_{name}_dram"] = a
        args.append(nc.dram_tensor(f"in_{name}_dram", a.shape, _mybir.dt.from_np(a.dtype), kind="ExternalInput").ap())
    for i, (shape, dtype) in enumerate(_OUTS):
        dt = _mybir.dt.from_np(_np.dtype(dtype))
        args.append(nc.dram_tensor(f"out_{i}_dram", shape, dt, kind="ExternalOutput").ap())
    fused_layer(nc, *args)
    r = _run(nc, [arrays], core_ids=[0])
    return r.results[0]["out_0_dram"]
```

```python
from contextlib import ExitStack

import concourse.bass as bass
from concourse import mybir

ALU = mybir.AluOpType
ACT = mybir.ActivationFunctionType
AX = mybir.AxisListType
F32 = mybir.dt.float32
F32R = mybir.dt.float32r
BF16 = mybir.dt.bfloat16

P = 128


def fused_layer(nc, x, w_in, w_gate, b_gate, amplitudes, sharpness, offsets, w1, w2, router_w, out):
    B, S, D = x.shape
    H, K = amplitudes.shape
    HD = D // H
    E, I2, _ = w1.shape
    I = I2 // 2
    T = B * S // P
    G = T // 4
    ST = S // P
    NPART = 3
    KC = NPART * NPART * HD
    VC = 32
    OC = HD + 1
    REL = 2 * S
    RC = REL // P
    BW = S + (ST - 1) * P
    EPS = 1e-5
    SCALE = 1.0 / float(HD) ** 0.5
    HIGHEST = 3.0e38
    SPLIT = 768
    UNITS = H * B
    TILES = UNITS * ST
    BODY = 2 * B * ST
    RING = 4
    SH_LAG = 2
    T_LAG, PV_LAG = 3, 12
    EV_LAG = PV_LAG + ST - 1
    OT_LAG = EV_LAG + 1

    qk_parts = nc.dram_tensor("qk_parts", (2, NPART, D, B * S), BF16).ap()
    qk_rows = nc.dram_tensor("qk_rows", (2, H, KC, B * S), BF16).ap()
    bias_dram = nc.dram_tensor("bias_rel", (H, REL), F32).ap()

    with ExitStack() as ctx:
        def sb(name, shape, dt=F32):
            return ctx.enter_context(nc.sbuf_tensor(name, shape, dt))

        def sem(name):
            return ctx.enter_context(nc.semaphore(name))

        ps = ctx.enter_context(nc.psum_tensor("ps", [P, 8, 512], F32))

        acc = sb("acc", [P, T, D])
        v_all = sb("v_all", [P, T, D])
        wg = sb("wg", [P, 2 * D])
        bg = sb("bg", [P, 2 * D])
        ident = sb("ident", [P, P])

        x_tok = x.rearrange("b s d -> (b s) d").rearrange("(t p) d -> p t d", p=P)
        out_tok = out.rearrange("b s d -> (b s) d").rearrange("(t p) d -> p t d", p=P)

        early = ctx.enter_context(ExitStack())

        def eb(name, shape, dt=F32):
            return early.enter_context(nc.sbuf_tensor(name, shape, dt))

        xh, xl = eb("xh", [P, T * P], F32R), eb("xl", [P, T * P], F32R)
        w1h, w1l = eb("w1h", [P, E, I2], F32R), eb("w1l", [P, E, I2], F32R)
        w2T = eb("w2T", [P, E, 2, D])
        comb = eb("comb", [P, T, E])
        gate_s = eb("gate_s", [P, 2, 512])
        y = eb("y", [P, 2, 2, 512])
        w1n = eb("w1n", [P, E, 4, D])
        w2n = eb("w2n", [P, E, I])
        wi = eb("wi", [P, 3 * D])
        flip = eb("flip", [P, P])
        xn = eb("xn", [P, 2, 4, D])
        xnT = eb("xnT", [P, 2, 512])
        xrev = eb("xrev", [P, 2, 512])
        resid = eb("resid", [P, 2, 512])
        parts = eb("parts", [P, 4, NPART, 512], BF16)
        par = eb("par", [P, 3, H * K])
        bt = eb("bt", [P, RC, H, K])
        bsum = eb("bsum", [P, RC, H])
        bsT = eb("bsT", [P, 2 * P])
        rel = eb("rel", [P, RC])
        stats = eb("stats", [P, T, 6])
        mv = eb("mv", [P, T, 2])
        std = eb("std", [P, T])
        rstd = eb("rstd", [P, T])
        eps = eb("eps", [P, 1])
        rtn = eb("rtn", [E, D])
        rT = eb("rT", [P, E])
        prio = eb("prio", [P, E])
        spare = y[:, :, :, :].rearrange("p a b c -> p (a b c)")
        small = spare[:, 0:7 * T * E].rearrange("p (n t e) -> p n t e", n=7, t=T)
        sm1 = spare[:, 7 * T * E:(7 * E + 6) * T].rearrange("p (n t) -> p n t", n=6)

        XG = G
        TG = T // XG
        s_x = [sem(f"x_loaded{i}") for i in range(XG)]
        s_win = sem("w_in_loaded")
        s_par = sem("bias_params_loaded")
        s_rt = sem("router_loaded")
        s_w1 = sem("w1_loaded")
        s_w2 = sem("w2_loaded")
        s_late = sem("gate_weights_loaded")
        s_eps = sem("eps_ready")
        s_id0 = sem("ident_zeroed")
        s_id = sem("ident_ready")
        s_fl = sem("flip_ready")
        s_xr = sem("xn_reversed")
        s_xrc = sem("xrev_copied")
        s_rel = sem("rel_ready")
        s_stats = sem("stats_done")
        s_mv = sem("mean_var_done")
        s_std = sem("std_done")
        s_rstd = sem("rstd_done")
        s_xn = sem("xn_done")
        s_xt = sem("xn_transposed")
        s_xte = sem("xnT_copied")
        s_qk = sem("qk_projected")
        s_p1 = sem("part1_done")
        s_r1 = sem("rest1_done")
        s_p2 = sem("part2_done")
        s_p3 = sem("part3_done")
        s_pst = [sem(f"parts_stored{i}") for i in range(4)]
        s_fill = sem("wide_filled")
        s_cp = sem("wide_copied")
        s_rtT = sem("router_transposed")
        s_rtc = sem("router_copied")
        s_log = sem("logits_done")
        s_dv = sem("router_step")
        s_re = sem("router_exp")
        s_d = sem("bias_distance")
        s_bq = sem("bias_square")
        s_bm = sem("bias_exponent")
        s_be = sem("bias_exp")
        s_ba = sem("bias_weighted")
        s_bs = sem("bias_summed")
        s_bT = sem("bias_transposed")
        s_bc = sem("bias_copied")
        s_bst = sem("bias_stored")

        s_gu = sem("gate_up_done")
        s_sg = sem("silu_done")
        s_y = sem("y_done")
        s_dn = sem("down_done")
        s_ac = sem("expert_added")
        s_row = sem("rows_stacked")
        s_xh = sem("x_high_done")
        s_xl = sem("x_rest_done")
        s_wl = sem("w1_rest_done")
        BQ = 4
        BIAS_STEP = 6

        def wait(eng, s, it, per, n):
            if isinstance(it, int):
                n, it = n + it * per, None
                if n <= 0:
                    return
            eng.wait_ge(s, n if it is None else it * per + n)

        def sweep(eng, times, body, lag, first, step):
            for k in range(first):
                step(0, k)
            with eng.Fori(0, times - 1) as it:
                for k in range(first, first + body):
                    step(it, k)
            for k in range(first, body + lag):
                step(times - 1, k)

        def tiles(it, k, s):
            n = (it + k // E) * 4 + s
            return slice(n, n + 1) if isinstance(it, int) else bass.ds(n, 1)

        def block_of(it, k):
            n = (it + k // E) * 512
            return slice(n, n + 512) if isinstance(it, int) else bass.ds(n, 512)

        def runs(it, k):
            return k >= 0 and (not isinstance(it, int) or it * E + k < G * E)

        def reversed_group(g):
            per = S // 512
            return g // per * per + per - 1 - g % per

        bt_flat = bt[:, :, :, :].rearrange("p c h k -> p c (h k)")
        with nc.Block() as block:
            @block.sync
            def _(sp):
                for i in range(XG):
                    sp.dma_start(acc[:, i * TG:(i + 1) * TG, :], x_tok[:, i * TG:(i + 1) * TG, :]).then_inc(s_x[i], 16)
                    if i == 0:
                        sp.dma_start(wi[:, :], w_in).then_inc(s_win, 16)
                for n, a in enumerate((amplitudes, sharpness, offsets)):
                    sp.dma_start(par[:, n, :], a.rearrange("h k -> (h k)").partition_broadcast(P)).then_inc(s_par, 16)
                sp.dma_start(rtn[:, :], router_w).then_inc(s_rt, 16)
                sp.dma_start(w1n[:, :, :, :], w1.rearrange("e (j p) d -> p e j d", p=P)).then_inc(s_w1, 16)
                sp.dma_start(w2n[:, :, :], w2.rearrange("e h i -> h e i")).then_inc(s_w2, 16)
                sp.dma_start(wg[:, :], w_gate).then_inc(s_late, 16)
                sp.dma_start(bg[:, :], b_gate.partition_broadcast(P)).then_inc(s_late, 16)
                for j in range(2 * G):
                    g, w = j // 2, j % 2
                    if w:
                        g = reversed_group(g)
                    sp.wait_ge(s_p3, j + 1)
                    sp.wait_ge(s_p2, j + 1)
                    sp.dma_start(qk_parts[w, :, :, g * 512:(g + 1) * 512].rearrange("n d t -> d n t"),
                                 parts[:, j % 4, :, :]).then_inc(s_pst[j % 4], 16)
                for a in s_pst:
                    sp.wait_ge(a, 16 * 2 * G // 4)
                stacked = qk_rows.rearrange("w h (n m d) t -> w n m h d t", n=NPART, m=NPART)
                for n in range(NPART):
                    for m in range(NPART):
                        for w in range(2):
                            src = qk_parts[w, m if w else n].rearrange("(h d) t -> h d t", d=HD)
                            sp.dma_start(stacked[w, n, m], src).then_inc(s_row, 16)
                sp.wait_ge(s_bc, 1)
                for n in range(2):
                    sp.dma_start(bias_dram.rearrange("h (c r) -> c h r", r=P)[8 * n:8 * n + 8],
                                 bsT[:, n * P:(n + 1) * P]).then_inc(s_bst, 16)
                sp.wait_ge(s_row, 16 * 2 * NPART * NPART)
                sp.wait_ge(s_bst, 32)
                sp.wait_ge(s_late, 32)

            @block.gpsimd
            def _(pool):
                nc.gpsimd.memset(eps[:, :], EPS).then_inc(s_eps, 1)
                nc.gpsimd.memset(ident[:, :], 0.0).then_inc(s_id0, 1)
                pool.wait_ge(s_id0, 1)
                nc.gpsimd.affine_select(out=ident[:, :], in_=ident[:, :], compare_op=ALU.not_equal, fill=1.0,
                                        base=0, pattern=[[-1, P]], channel_multiplier=1).then_inc(s_id, 1)
                nc.gpsimd.memset(flip[:, :], 0.0).then_inc(s_fl, 1)
                pool.wait_ge(s_fl, 1)
                nc.gpsimd.affine_select(out=flip[:, :], in_=flip[:, :], compare_op=ALU.not_equal, fill=1.0,
                                        base=-(P - 1), pattern=[[1, P]], channel_multiplier=1).then_inc(s_fl, 1)
                nc.gpsimd.iota(rel[:, :], pattern=[[-P, RC]], base=S - 1, channel_multiplier=-1,
                               allow_small_or_imprecise_dtypes=True).then_inc(s_rel, 1)
                nc.gpsimd.iota(prio[:, :], pattern=[[-1, E]], base=E, channel_multiplier=0,
                               allow_small_or_imprecise_dtypes=True).then_inc(s_rel, 1)
                for c in range(RC + 1):
                    if c < RC:
                        pool.wait_ge(s_d, c + 2)
                        nc.gpsimd.tensor_tensor(bt_flat[:, c, :], bt_flat[:, c, :], bt_flat[:, c, :],
                                                ALU.mult).then_inc(s_bq, 1)
                    if c:
                        pool.wait_ge(s_bq, c)
                        nc.gpsimd.tensor_tensor(bt_flat[:, c - 1, :], bt_flat[:, c - 1, :], par[:, 1, :],
                                                ALU.mult).then_inc(s_bm, 1)
                for c in range(RC):
                    pool.wait_ge(s_be, c + 1)
                    nc.gpsimd.tensor_tensor(bt_flat[:, c, :], bt_flat[:, c, :], par[:, 0, :],
                                            ALU.mult).then_inc(s_ba, 1)

            @block.vector
            def _(dve):
                def statistics(i):
                    dve.wait_ge(s_x[i], 16)
                    for t in range(i * TG, (i + 1) * TG):
                        nc.vector.bn_stats(stats[:, t, :], acc[:, t, :]).then_inc(s_stats, 1)
                    for t in range(i * TG, (i + 1) * TG):
                        dve.wait_ge(s_stats, t + 1)
                        nc.vector.bn_aggr(mv[:, t, :], stats[:, t, :]).then_inc(s_mv, 1)

                def normalise(i):
                    dve.wait_ge(s_std, i + 1)
                    nc.vector.reciprocal(rstd[:, i * TG:(i + 1) * TG], std[:, i * TG:(i + 1) * TG]).then_inc(s_rstd, 1)
                    dve.wait_ge(s_rstd, i + 1)
                    if i >= 2:
                        dve.wait_ge(s_xt, i - 1)
                        dve.wait_ge(s_xr, i - 1)
                    for t in range(i * TG, (i + 1) * TG):
                        nc.vector.tensor_scalar(xn[:, i % 2, t % 4, :], acc[:, t, :], mv[:, t, 0:1], rstd[:, t:t + 1],
                                                ALU.subtract, ALU.mult).then_inc(s_xn, 1)

                statistics(0)
                for i in range(1, XG):
                    statistics(i)
                    if i == 1:
                        normalise(0)
                normalise(1)

                dve.wait_ge(s_rtT, 1)
                nc.vector.tensor_copy(rT[:, :], ps[:, 6, 0:E]).then_inc(s_rtc, 1)

                def distances():
                    dve.wait_ge(s_par, 48)
                    dve.wait_ge(s_rel, 2)
                    nc.vector.scalar_tensor_tensor(out=par[:, 1, :], in0=par[:, 1, :], scalar=-1.0, in1=par[:, 1, :],
                                                   op0=ALU.mult, op1=ALU.max).then_inc(s_d, 1)
                    for c in range(RC):
                        nc.vector.tensor_scalar(bt_flat[:, c, :], par[:, 2, :], rel[:, c:c + 1], None,
                                                ALU.subtract).then_inc(s_d, 1)

                def first_rest(j):
                    dve.wait_ge(s_p1, j + 1)
                    if j >= 2:
                        dve.wait_ge(s_p3, j - 1)
                    sc = SCALE if j % 2 == 0 else 1.0
                    nc.vector.scalar_tensor_tensor(out=resid[:, j % 2, :], in0=ps[:, 2 + j % 2, :], scalar=sc,
                                                   in1=parts[:, j % 4, 0, :], op0=ALU.mult,
                                                   op1=ALU.subtract).then_inc(s_r1, 1)

                def last_part(j):
                    dve.wait_ge(s_p2, j + 1)
                    nc.vector.tensor_tensor(parts[:, j % 4, 2, :], resid[:, j % 2, :], parts[:, j % 4, 1, :],
                                            ALU.subtract).then_inc(s_p3, 1)

                def x_rest(g):
                    dve.wait_ge(s_xh, g + 1)
                    cols = slice(g * 512, (g + 1) * 512)
                    nc.vector.tensor_tensor(xl[:, cols], ps[:, g % 2, :], xh[:, cols].bitcast(F32),
                                            ALU.subtract).then_inc(s_xl, 1)

                def w1_rest(e):
                    dve.wait_ge(s_cp, 2 * e + 2)
                    nc.vector.tensor_tensor(w1l[:, e, :], ps[:, 5, :], w1h[:, e, :].bitcast(F32),
                                            ALU.subtract).then_inc(s_wl, 1)

                for g in range(G):
                    x_rest(g)
                    first_rest(2 * g)
                    if g:
                        last_part(2 * g - 1)
                    if g + 2 < G:
                        normalise(g + 2)
                    first_rest(2 * g + 1)
                    last_part(2 * g)
                    if g == 1:
                        distances()
                    w1_rest(g)
                last_part(2 * G - 1)

                logits = ps[:, 6, 0:T * E].rearrange("p (t e) -> p t e", e=E)
                lg, pr, eq, sel1, rest, eq2, sel2 = (small[:, n] for n in range(7))
                mx, sm, rs, top, mxr, top2 = (sm1[:, n] for n in range(6))

                def bc(a):
                    return a.unsqueeze(2).to_broadcast([P, T, E])

                done = [0]

                def step(ins):
                    done[0] += 1
                    ins.then_inc(s_dv, 1)
                    dve.wait_ge(s_dv, done[0])

                pri = prio[:, :].unsqueeze(1).to_broadcast([P, T, E])
                dve.wait_ge(s_log, G)
                step(nc.vector.tensor_reduce(mx, logits, AX.X, ALU.max))
                step(nc.vector.tensor_tensor(lg, logits, bc(mx), ALU.subtract))
                dve.wait_ge(s_re, 1)
                step(nc.vector.tensor_reduce(sm, pr, AX.X, ALU.add))
                step(nc.vector.reciprocal(rs, sm))
                step(nc.vector.tensor_tensor(pr, pr, bc(rs), ALU.mult))
                step(nc.vector.tensor_reduce(mx, pr, AX.X, ALU.max))
                step(nc.vector.tensor_tensor(eq, pr, bc(mx), ALU.is_equal))
                step(nc.vector.tensor_tensor(eq, eq, pri, ALU.mult))
                step(nc.vector.tensor_reduce(top, eq, AX.X, ALU.max))
                step(nc.vector.tensor_tensor(sel1, eq, bc(top), ALU.is_equal))
                step(nc.vector.scalar_tensor_tensor(out=rest, in0=sel1, scalar=-2.0, in1=pr, op0=ALU.mult, op1=ALU.add))
                step(nc.vector.tensor_reduce(mxr, rest, AX.X, ALU.max))
                step(nc.vector.tensor_tensor(eq2, rest, bc(mxr), ALU.is_equal))
                step(nc.vector.tensor_tensor(eq2, eq2, pri, ALU.mult))
                step(nc.vector.tensor_reduce(top2, eq2, AX.X, ALU.max))
                step(nc.vector.tensor_tensor(sel2, eq2, bc(top2), ALU.is_equal))
                step(nc.vector.tensor_tensor(sel1, sel1, sel2, ALU.add))
                step(nc.vector.tensor_tensor(comb[:, :, :], sel1, pr, ALU.mult))

                def multiply(it, k):
                    for half in range(2):
                        n = 2 * k + half
                        wait(dve, s_sg, it, 2 * E, n + 1)
                        wait(dve, s_gu, it, 4 * E, 2 * n + 2)
                        wait(dve, s_dn, it, E, k - 1)
                        nc.vector.tensor_tensor(y[:, k % 2, half, :], ps[:, 2 * half + 1, :], gate_s[:, half, :],
                                                ALU.mult).then_inc(s_y, 1)

                def add(it, k):
                    wait(dve, s_dn, it, E, k + 1)
                    for s in range(4):
                        wait(dve, s_ac, it, 4 * E, 4 * (k - 1) + s + 1)
                        a = acc[:, tiles(it, k, s), :].rearrange("p a d -> p (a d)")
                        w = comb[:, tiles(it, k, s), k % E:k % E + 1].rearrange("p a d -> p (a d)")
                        nc.vector.scalar_tensor_tensor(out=a, in0=ps[:, 4 + k % 2, s * P:(s + 1) * P], scalar=w,
                                                       in1=a, op0=ALU.mult, op1=ALU.add).then_inc(s_ac, 1)

                def bias_sum(q):
                    dve.wait_ge(s_ba, RC)
                    c = slice(q * RC // BQ, (q + 1) * RC // BQ)
                    nc.vector.tensor_reduce(bsum[:, c, :], bt[:, c, :, :], AX.X, ALU.add).then_inc(s_bs, 1)

                def step(it, k):
                    if runs(it, k):
                        multiply(it, k)
                    if runs(it, k - 1):
                        add(it, k - 1)
                    if isinstance(it, int) and it:
                        if BIAS_STEP - BQ <= k - 1 < BIAS_STEP:
                            bias_sum(k - 1 - (BIAS_STEP - BQ))
                        if k == BIAS_STEP + 2:
                            dve.wait_ge(s_bT, 1)
                            nc.vector.tensor_copy(bsT[:, :], ps[:, 7, 0:2 * P]).then_inc(s_bc, 1)

                sweep(dve, G, E, 1, 3, step)

            @block.scalar
            def _(act):
                for i in range(XG):
                    act.wait_ge(s_mv, (i + 1) * TG)
                    act.wait_ge(s_eps, 1)
                    nc.scalar.activation(std[:, i * TG:(i + 1) * TG], mv[:, i * TG:(i + 1) * TG, 1], ACT.Sqrt,
                                         bias=eps[:, 0:1], scale=1.0).then_inc(s_std, 1)

                def xnT_copy(g):
                    act.wait_ge(s_xt, g + 1)
                    if g >= 2:
                        act.wait_ge(s_qk, 2 * g - 3)
                        act.wait_ge(s_log, g - 1)
                    nc.scalar.copy(xnT[:, g % 2, :], ps[:, g % 2, :]).then_inc(s_xte, 1)
                    nc.scalar.copy(xh[:, g * 512:(g + 1) * 512], ps[:, g % 2, :]).then_inc(s_xh, 1)

                def xrev_copy(g):
                    act.wait_ge(s_xr, g + 1)
                    if g >= 2:
                        act.wait_ge(s_qk, 2 * g - 2)
                        act.wait_ge(s_fill, 2 * g - 3)
                    nc.scalar.copy(xrev[:, g % 2, :], ps[:, 7, :]).then_inc(s_xrc, 1)

                def first_part(j):
                    act.wait_ge(s_qk, j + 1)
                    if j >= 4:
                        act.wait_ge(s_pst[j % 4], 16 * (j // 4))
                    sc = SCALE if j % 2 == 0 else 1.0
                    nc.scalar.mul(parts[:, j % 4, 0, :], ps[:, 2 + j % 2, :], sc).then_inc(s_p1, 1)

                def second_part(j):
                    act.wait_ge(s_r1, j + 1)
                    nc.scalar.copy(parts[:, j % 4, 1, :], resid[:, j % 2, :]).then_inc(s_p2, 1)

                def wide_copy(n):
                    act.wait_ge(s_fill, n + 1)
                    src = ps[:, 4 + n % 2, :]
                    if n >= 2 * G:
                        m = n - 2 * G
                        nc.scalar.copy(w2T[:, 2 * m:2 * m + 2, :, :].rearrange("p e i d -> p (e i d)"),
                                       src).then_inc(s_cp, 1)
                    elif n % 2:
                        nc.scalar.copy(w1h[:, n // 2, :], src).then_inc(s_cp, 1)
                    else:
                        k = 4 * reversed_group(n // 2)
                        nc.scalar.copy(v_all[:, k:k + 4, :].rearrange("p t d -> p (t d)"), src).then_inc(s_cp, 1)

                def bias_exp(c):
                    act.wait_ge(s_bm, c + 1)
                    nc.scalar.activation(bt_flat[:, c, :], bt_flat[:, c, :], ACT.Exp, scale=-1.0).then_inc(s_be, 1)

                xnT_copy(0)
                xrev_copy(0)
                for g in range(G):
                    if g + 1 < G:
                        xnT_copy(g + 1)
                        xrev_copy(g + 1)
                    first_part(2 * g)
                    if g:
                        second_part(2 * g - 1)
                    first_part(2 * g + 1)
                    second_part(2 * g)
                    wide_copy(2 * g)
                    wide_copy(2 * g + 1)
                    if g >= G - 4:
                        for c in range(4 * (g - G + 4), 4 * (g - G + 4) + 4):
                            bias_exp(c)
                second_part(2 * G - 1)
                for n in range(2 * G, 2 * G + E // 2):
                    wide_copy(n)
                act.wait_ge(s_dv, 2)
                nc.scalar.activation(small[:, 1], small[:, 0], ACT.Exp).then_inc(s_re, 1)

                def step(it, k):
                    for half in range(2):
                        n = 2 * k + half
                        wait(act, s_gu, it, 4 * E, 2 * n + 1)
                        wait(act, s_y, it, 2 * E, n - 1)
                        nc.scalar.activation(gate_s[:, half, :], ps[:, 2 * half, :], ACT.Silu).then_inc(s_sg, 1)

                sweep(act, G, E, 0, 2, step)

            @block.tensor
            def _(pe):
                pe.wait_ge(s_id, 1)
                pe.wait_ge(s_rt, 16)
                nc.tensor.transpose(ps[:, 6, 0:E], rtn[:, :], ident[0:E, 0:E]).then_inc(s_rtT, 1)

                def turn_xn(g):
                    pe.wait_ge(s_xn, 4 * g + 4)
                    if g >= 2:
                        pe.wait_ge(s_xte, g - 1)
                        pe.wait_ge(s_xh, g - 1)
                        pe.wait_ge(s_xl, g - 1)
                    for t in range(4):
                        mm = nc.tensor.transpose(ps[:, g % 2, t * P:(t + 1) * P], xn[:, g % 2, t, :], ident[:, :])
                    mm.then_inc(s_xt, 1)

                def turn_reversed(g):
                    if g >= 1:
                        pe.wait_ge(s_xrc, g)
                    for t in range(4):
                        mm = nc.tensor.transpose(ps[:, 7, (3 - t) * P:(4 - t) * P], xn[:, g % 2, t, :], flip[:, :])
                    mm.then_inc(s_xr, 1)

                def project(j):
                    g, w = j // 2, j % 2
                    pe.wait_ge(s_xrc if w else s_xte, g + 1)
                    if j >= 2:
                        pe.wait_ge(s_p1, j - 1)
                        pe.wait_ge(s_r1, j - 1)
                    col = 2 * D if w == 0 else 0
                    tokens = xrev[:, g % 2, :] if w else xnT[:, g % 2, :]
                    nc.tensor.matmul(ps[:, 2 + j % 2, :], wi[:, col:col + D], tokens,
                                     start=True, stop=True).then_inc(s_qk, 1)

                def route(g):
                    for t in range(4):
                        k = 4 * g + t
                        mm = nc.tensor.matmul(ps[:, 6, k * E:(k + 1) * E], xnT[:, g % 2, t * P:(t + 1) * P], rT[:, :],
                                              start=True, stop=True)
                    mm.then_inc(s_log, 1)

                def wide(n):
                    if n >= 2:
                        pe.wait_ge(s_cp, n - 1)
                    if n % 2 and n >= 3:
                        pe.wait_ge(s_wl, min(n // 2, E))
                    for t in range(4):
                        dst = ps[:, 4 + n % 2, t * P:(t + 1) * P]
                        if n >= 2 * G:
                            e = 2 * (n - 2 * G) + t // 2
                            mm = nc.tensor.transpose(dst, w2n[:, e, t % 2 * P:(t % 2 + 1) * P], ident[:, :])
                        elif n % 2:
                            mm = nc.tensor.transpose(dst, w1n[:, n // 2, t, :], ident[:, :])
                        else:
                            mm = nc.tensor.matmul(dst, xrev[:, n // 2 % 2, t * P:(t + 1) * P], wi[:, D:2 * D],
                                                  start=True, stop=True)
                    mm.then_inc(s_fill, 1)

                turn_xn(0)
                pe.wait_ge(s_fl, 2)
                turn_reversed(0)
                pe.wait_ge(s_win, 16)
                pe.wait_ge(s_rtc, 1)
                for g in range(G):
                    if g + 1 < G:
                        turn_xn(g + 1)
                        turn_reversed(g + 1)
                    project(2 * g)
                    project(2 * g + 1)
                    wide(2 * g)
                    route(g)
                    if g == 0:
                        pe.wait_ge(s_w1, 16)
                    wide(2 * g + 1)
                pe.wait_ge(s_w2, 16)
                for n in range(2 * G, 2 * G + E // 2):
                    wide(n)
                pe.wait_ge(s_xl, G)
                pe.wait_ge(s_xh, G)
                pe.wait_ge(s_p1, 2 * G)
                pe.wait_ge(s_r1, 2 * G)
                pe.wait_ge(s_cp, 2 * G + E // 2)
                pe.wait_ge(s_xrc, G)

                def gate_up(it, k):
                    e = k % E
                    for half in range(2):
                        n = 2 * k + half
                        wait(pe, s_y, it, 2 * E, n - 1)
                        for u in range(2):
                            cols = slice(u * I + half * P, u * I + half * P + P)
                            dst, blk = ps[:, 2 * half + u, :], block_of(it, k)
                            nc.tensor.matmul(dst, w1h[:, e, cols], xh[:, blk], start=True, stop=False)
                            nc.tensor.matmul(dst, w1h[:, e, cols], xl[:, blk], start=False, stop=False)
                            nc.tensor.matmul(dst, w1l[:, e, cols], xh[:, blk],
                                             start=False, stop=True).then_inc(s_gu, 1)

                def down(it, k):
                    wait(pe, s_y, it, 2 * E, 2 * k + 2)
                    wait(pe, s_ac, it, 4 * E, 4 * (k - 1))
                    for s in range(4):
                        for half in range(2):
                            mm = nc.tensor.matmul(ps[:, 4 + k % 2, s * P:(s + 1) * P],
                                                  y[:, k % 2, half, s * P:(s + 1) * P], w2T[:, k % E, half, :],
                                                  start=(half == 0), stop=(half == 1))
                    mm.then_inc(s_dn, 1)

                def turn_bias():
                    pe.wait_ge(s_bs, BQ)
                    bflat = bsum[:, :, :].rearrange("p c h -> p (c h)")
                    for n in range(2):
                        mm = nc.tensor.transpose(ps[:, 7, n * P:(n + 1) * P], bflat[:, n * P:(n + 1) * P], ident[:, :])
                    mm.then_inc(s_bT, 1)

                def step(it, k):
                    if runs(it, k):
                        gate_up(it, k)
                    if runs(it, k - 1):
                        down(it, k - 1)
                    if isinstance(it, int) and it and k == BIAS_STEP + 1:
                        turn_bias()

                sweep(pe, G, E, 1, 3, step)

        early.close()

        pT = sb("pT", [P, 2, ST, S])
        shifted = sb("shifted", [P, RING, S])
        bias = sb("bias", [P, 2, BW])
        qs = sb("qs", [KC, 2, S], BF16)
        ks = sb("ks", [KC, 2, S], BF16)
        vu = sb("vu", [P, 2, ST, VC])
        negmax = sb("negmax", [P, 8])
        oT = sb("oT", [P, 2 * P])
        o_all = sb("o_all", [P, T, H, OC])
        s_vz = sem("v_zeroed")
        s_ql = [sem(f"qk_loaded{i}") for i in range(2)]
        s_bl = [sem(f"bias_loaded{i}") for i in range(2)]
        s_vc = sem("v_copied")
        s_s = sem("scores_done")
        s_m = sem("max_done")
        s_sh = sem("shift_done")
        s_sha = sem("shift_by_act_done")
        s_tr = sem("half_transposed")
        s_e = sem("half_exped")
        s_pv = sem("pv_piece_done")
        s_ev = sem("out_copied")
        s_ot = sem("out_transposed")
        s_oc = sem("out_kept")
        o_tiles = o_all[:, :, :, :].rearrange("p (b j s) h c -> p s b j h c", b=B, j=4, s=2)

        def within(it, k):
            return k >= 0 and (not isinstance(it, int) or it * BODY + k < TILES)

        LOADS = 2
        U = BODY // ST
        with nc.Block() as block:
            @block.sync
            def _(sp):
                def load_unit(it, u):
                    wait(sp, s_s, it, BODY, ST * (u - 1))
                    h = it * 2 + u // B
                    b = u % B
                    col = slice(b * S, (b + 1) * S)
                    for w, dst in enumerate((qs, ks)):
                        src = qk_rows[w, h, :, col] if isinstance(it, int) else \
                            qk_rows[w, bass.ds(h, 1), :, col].rearrange("a r t -> (a r) t")
                        sp.dma_start(dst[:, u % 2, :], src).then_inc(s_ql[u % 2], 16)

                def load_bias(it, hh):
                    wait(sp, s_m, it, BODY, B * ST * (hh - 1))
                    h = it * 2 + hh
                    row = bias_dram[h, :] if isinstance(it, int) else bias_dram[bass.ds(h, 1), :]
                    src = bass.AP(row.tensor, row.offset, [[1, P], [1, BW]])
                    sp.dma_start(bias[:, hh % 2, :], src).then_inc(s_bl[hh % 2], 16)

                load_bias(0, 0)
                load_unit(0, 0)
                load_unit(0, 1)
                load_bias(0, 1)
                with sp.Fori(0, TILES // BODY - 1) as it:
                    for u in range(2, U + 2):
                        load_unit(it, u)
                        if u == B + 1:
                            load_bias(it, 2)
                    load_bias(it, 3)
                for u in range(2, U):
                    load_unit(TILES // BODY - 1, u)

            @block.gpsimd
            def _(pool):
                def copy_v(it, u):
                    wait(pool, s_pv, it, BODY, ST * (u - 1))
                    h = it * 2 + u // B
                    b = u % B
                    cols = slice(h * HD, (h + 1) * HD) if isinstance(it, int) else bass.ds(h * HD, HD)
                    nc.gpsimd.tensor_copy(vu[:, u % 2, :, 0:HD], v_all[:, b * ST:(b + 1) * ST, cols]).then_inc(s_vc, 1)

                nc.gpsimd.memset(vu[:, :, :, :], 0.0).then_inc(s_vz, 1)
                pool.wait_ge(s_vz, 1)
                nc.gpsimd.memset(vu[:, :, :, HD:HD + 1], 1.0).then_inc(s_vz, 1)
                pool.wait_ge(s_vz, 2)
                copy_v(0, 0)
                copy_v(0, 1)
                with pool.Fori(0, TILES // BODY - 1) as it:
                    for u in range(2, U + 2):
                        copy_v(it, u)
                for u in range(2, U):
                    copy_v(TILES // BODY - 1, u)

            @block.tensor
            def _(pe):
                def scores(it, k):
                    u = k // ST
                    if k % ST == 0:
                        wait(pe, s_ql[u % 2], it, 16 * LOADS * U // 2, 16 * LOADS * (u // 2 + 1))
                    wait(pe, s_m, it, BODY, k - 1)
                    for n in range(2):
                        mm = nc.tensor.matmul(ps[:, 2 * (k % 2) + n, :], qs[:, u % 2, (k % ST) * P:(k % ST + 1) * P],
                                              ks[:, u % 2, n * 512:(n + 1) * 512], start=True, stop=True)
                    mm.then_inc(s_s, 1)

                def turn(it, k, half):
                    wait(pe, s_sha if half else s_sh, it, BODY, k + 1)
                    wait(pe, s_e, it, 2 * BODY, 2 * k + half - 1)
                    for c in range(4):
                        col = (4 * half + c) * P
                        mm = nc.tensor.transpose(ps[:, 4 + half, c * P:(c + 1) * P],
                                                 shifted[:, k % RING, col:col + P], ident[:, :])
                    mm.then_inc(s_tr, 1)

                def weigh(it, k):
                    u, kt = k // ST, k % ST
                    if kt == 0:
                        wait(pe, s_e, it, 2 * BODY, 2 * ST * (u + 1))
                        wait(pe, s_vc, it, U, u + 1)
                        wait(pe, s_ev, it, U, u)
                    for j in range(4):
                        mm = nc.tensor.matmul(ps[32 * j:32 * j + 32, 6, 0:256], vu[:, u % 2, kt, :],
                                              pT[:, u % 2, kt, j * 256:(j + 1) * 256],
                                              start=(kt == 0), stop=(kt == ST - 1), tile_position=(0, 32 * j))
                    mm.then_inc(s_pv, 1)

                def turn_out(it, u):
                    wait(pe, s_ev, it, U, u + 1)
                    wait(pe, s_oc, it, U, u)
                    for s in range(2):
                        mm = nc.tensor.transpose(ps[:, 7, s * P:(s + 1) * P], oT[:, s * P:(s + 1) * P], ident[:, :])
                    mm.then_inc(s_ot, 1)

                def step(it, k):
                    if within(it, k):
                        scores(it, k)
                    if within(it, k - T_LAG):
                        turn(it, k - T_LAG, 0)
                    if within(it, k - PV_LAG):
                        weigh(it, k - PV_LAG)
                    if within(it, k - T_LAG):
                        turn(it, k - T_LAG, 1)
                    if k >= OT_LAG and (k - OT_LAG) % ST == 0:
                        turn_out(it, (k - OT_LAG) // ST)

                sweep(pe, TILES // BODY, BODY, PV_LAG + 1, OT_LAG + 1, step)

            @block.vector
            def _(dve):
                def may_add(it, k):
                    if k % (B * ST) == 0:
                        hh = k // (B * ST)
                        wait(dve, s_bl[hh % 2], it, 16, 16 * (hh // 2 + 1))
                    wait(dve, s_s, it, BODY, k + 1)
                    wait(dve, s_tr, it, 2 * BODY, 2 * (k - RING) + 2)

                def add_max(it, k):
                    off = (k % ST) * P
                    nc.vector.tensor_tensor_reduce(
                        shifted[:, k % RING, :],
                        ps[:, 2 * (k % 2):2 * (k % 2) + 2, :].rearrange("p a b -> p (a b)"),
                        bias[:, (k // (B * ST)) % 2, off:off + S], -1.0, HIGHEST, ALU.add, ALU.min,
                        negmax[:, k % 8:k % 8 + 1]).then_inc(s_m, 1)

                def shift(it, k):
                    wait(dve, s_m, it, BODY, k + 1)
                    nc.vector.tensor_scalar(shifted[:, k % RING, 0:SPLIT], shifted[:, k % RING, 0:SPLIT], -1.0,
                                            negmax[:, k % 8:k % 8 + 1], ALU.mult, ALU.add).then_inc(s_sh, 1)

                def step(it, k):
                    if within(it, k):
                        may_add(it, k)
                    if within(it, k - SH_LAG):
                        shift(it, k - SH_LAG)
                    if within(it, k):
                        add_max(it, k)

                sweep(dve, TILES // BODY, BODY, SH_LAG, ST, step)

            @block.scalar
            def _(act):
                def shift(it, k):
                    wait(act, s_m, it, BODY, k + 1)
                    rest = shifted[:, k % RING, SPLIT:S]
                    nc.scalar.activation(rest, rest, ACT.Identity, bias=negmax[:, k % 8:k % 8 + 1],
                                         scale=-1.0).then_inc(s_sha, 1)

                def expo(it, k, half):
                    u = k // ST
                    wait(act, s_tr, it, 2 * BODY, 2 * k + half + 1)
                    if k % ST == 0:
                        wait(act, s_pv, it, BODY, ST * (u - 1))
                    q = (k % ST) * P
                    nc.scalar.activation(pT[:, u % 2, 4 * half:4 * half + 4, q:q + P],
                                         ps[:, 4 + half, :].rearrange("p (a b) -> p a b", a=4),
                                         ACT.Exp).then_inc(s_e, 1)

                def keep_sum(it, u):
                    wait(act, s_pv, it, BODY, ST * (u + 1))
                    wait(act, s_ot, it, U, u)
                    nc.scalar.copy(oT[:, :], ps[:, 6, 0:256]).then_inc(s_ev, 1)

                def keep_out(it, u):
                    wait(act, s_ot, it, U, u + 1)
                    b = u % B
                    h = it * 2 + u // B
                    for s in range(2):
                        src = ps[:, 7, s * P:(s + 1) * P].rearrange("p (j c) -> p j c", j=4)[:, :, 0:OC]
                        if isinstance(it, int):
                            dst = o_tiles[:, s, b, :, h, :]
                        else:
                            dst = o_tiles[:, s, b, :, bass.ds(h, 1), :].rearrange("p j a c -> p j (a c)")
                        ins = nc.scalar.copy(dst, src)
                    ins.then_inc(s_oc, 1)

                def step(it, k):
                    if within(it, k - SH_LAG):
                        shift(it, k - SH_LAG)
                    if within(it, k - T_LAG):
                        expo(it, k - T_LAG, 0)
                    if k >= EV_LAG and (k - EV_LAG) % ST == 0:
                        keep_sum(it, (k - EV_LAG) // ST)
                    if within(it, k - T_LAG):
                        expo(it, k - T_LAG, 1)
                    if k >= OT_LAG and (k - OT_LAG) % ST == 0:
                        keep_out(it, (k - OT_LAG) // ST)

                sweep(act, TILES // BODY, BODY, PV_LAG + 1, OT_LAG, step)

        arena = pT[:, :, :, :].rearrange("p a b c -> p (a b c)")
        attn = arena[:, 0:4096].rearrange("p (t d) -> p t d", d=D)
        attnT = arena[:, 4096:8192]
        gated = arena[:, 8192:8192 + 3 * 512].rearrange("p (a t c) -> p a t c", a=3, t=2)
        sig = arena[:, 9728:9728 + 768].rearrange("p (a t c) -> p a t c", a=3, t=2)
        rsum = arena[:, 10496:10496 + T * H].rearrange("p (t h) -> p t h", t=T)
        s_rc = sem("sums_inverted")
        s_an = sem("attn_normalised")
        s_at = sem("attn_transposed")
        s_atc = sem("attnT_copied")
        s_gt = sem("gate_projected")
        s_gb = sem("gate_biased")
        s_si = sem("sigmoid_done")
        s_ml = sem("gated_done")
        s_fi = sem("result_done")
        s_out = sem("result_stored")
        NP2 = T // 2
        with nc.Block() as block:
            @block.vector
            def _(dve):
                nc.vector.reciprocal(rsum, o_all[:, :, :, HD]).then_inc(s_rc, 1)
                dve.wait_ge(s_rc, 1)

                def norm(g):
                    t = slice(4 * g, 4 * g + 4)
                    nc.vector.tensor_tensor(attn[:, t, :].rearrange("p t (h c) -> p (t h) c", c=HD),
                                            o_all[:, t, :, 0:HD].rearrange("p t h c -> p (t h) c"),
                                            rsum[:, t, :].rearrange("p t h -> p (t h)").unsqueeze(2)
                                            .to_broadcast([P, 4 * H, HD]), ALU.mult).then_inc(s_an, 1)

                def biased(n):
                    dve.wait_ge(s_gt, n + 1)
                    if n >= 3:
                        dve.wait_ge(s_ml, n - 2)
                    nc.vector.tensor_tensor(gated[:, n % 3], ps[:, 4 + n % 2, :].rearrange("p (t c) -> p t c", t=2),
                                            bg[:, :].unsqueeze(1).to_broadcast([P, 2, 2 * D]),
                                            ALU.add).then_inc(s_gb, 1)

                def final(n):
                    dve.wait_ge(s_ml, n + 1)
                    a = acc[:, 2 * n:2 * n + 2, :]
                    nc.vector.tensor_tensor(a, a, sig[:, n % 3], ALU.add).then_inc(s_fi, 1)

                norm(0)
                norm(1)
                for n in range(NP2 + 2):
                    if n % 2 == 0 and n // 2 + 2 < G:
                        norm(n // 2 + 2)
                    if n < NP2:
                        biased(n)
                    if n >= 2:
                        final(n - 2)

            @block.gpsimd
            def _(pool):
                for n in range(NP2):
                    pool.wait_ge(s_si, n + 1)
                    nc.gpsimd.tensor_tensor(sig[:, n % 3], gated[:, n % 3, :, 0:D], sig[:, n % 3],
                                            ALU.mult).then_inc(s_ml, 1)

            @block.scalar
            def _(act):
                def copy_t(g):
                    act.wait_ge(s_at, g + 1)
                    nc.scalar.copy(attnT[:, g * 512:(g + 1) * 512], ps[:, g % 2, :]).then_inc(s_atc, 1)

                copy_t(0)
                for n in range(NP2):
                    if n % 2 == 0 and n // 2 + 1 < G:
                        copy_t(n // 2 + 1)
                    act.wait_ge(s_gb, n + 1)
                    if n >= 3:
                        act.wait_ge(s_fi, n - 2)
                    nc.scalar.activation(sig[:, n % 3], gated[:, n % 3, :, D:2 * D], ACT.Sigmoid).then_inc(s_si, 1)

            @block.tensor
            def _(pe):
                def turn_attn(g):
                    pe.wait_ge(s_an, g + 1)
                    if g >= 2:
                        pe.wait_ge(s_atc, g - 1)
                    for t in range(4):
                        mm = nc.tensor.transpose(ps[:, g % 2, t * P:(t + 1) * P], attn[:, 4 * g + t, :], ident[:, :])
                    mm.then_inc(s_at, 1)

                turn_attn(0)
                for n in range(NP2):
                    if n % 2 == 0:
                        if n // 2 + 1 < G:
                            turn_attn(n // 2 + 1)
                        pe.wait_ge(s_atc, n // 2 + 1)
                    if n >= 2:
                        pe.wait_ge(s_gb, n - 1)
                    for t in range(2):
                        k = 2 * n + t
                        mm = nc.tensor.matmul(ps[:, 4 + n % 2, t * 2 * D:(t + 1) * 2 * D],
                                              attnT[:, k * P:(k + 1) * P], wg[:, :], start=True, stop=True)
                    mm.then_inc(s_gt, 1)

            @block.sync
            def _(sp):
                for g in range(G):
                    sp.wait_ge(s_fi, 2 * g + 2)
                    sp.dma_start(out_tok[:, 4 * g:4 * g + 4, :], acc[:, 4 * g:4 * g + 4, :]).then_inc(s_out, 16)
                sp.wait_ge(s_out, 16 * G)


_INS = ['L0_attn_x', 'L0_attn_w_in', 'L0_attn_w_gate', 'L0_attn_b_gate', 'L0_attn_amplitudes', 'L0_attn_sharpness',
        'L0_attn_offsets', 'L0_ffn_w1', 'L0_ffn_w2', 'L0_ffn_router_w']
_OUTS = [((4, 1024, 128), 'float32')]


def kernel(**inputs):
    import numpy as _np
    import concourse.bacc as _bacc
    from concourse import mybir as _mybir
    from concourse.bass_utils import run_bass_kernel_spmd as _run

    nc = _bacc.Bacc("TRN2", target_bir_lowering=False, num_devices=1)
    arrays, args = {}, []
    for name in _INS:
        a = _np.ascontiguousarray(inputs[name])
        arrays[f"in_{name}_dram"] = a
        args.append(nc.dram_tensor(f"in_{name}_dram", a.shape, _mybir.dt.from_np(a.dtype), kind="ExternalInput").ap())
    for i, (shape, dtype) in enumerate(_OUTS):
        dt = _mybir.dt.from_np(_np.dtype(dtype))
        args.append(nc.dram_tensor(f"out_{i}_dram", shape, dt, kind="ExternalOutput").ap())
    fused_layer(nc, *args)
    r = _run(nc, [arrays], core_ids=[0])
    return r.results[0]["out_0_dram"]
```

```python
from contextlib import ExitStack

import concourse.bass as bass
from concourse import mybir

ALU = mybir.AluOpType
ACT = mybir.ActivationFunctionType
AX = mybir.AxisListType
F32 = mybir.dt.float32
F32R = mybir.dt.float32r
BF16 = mybir.dt.bfloat16

P = 128


def fused_layer(nc, x, w_in, w_gate, b_gate, amplitudes, sharpness, offsets, w1, w2, router_w, out):
    B, S, D = x.shape
    H, K = amplitudes.shape
    HD = D // H
    E, I2, _ = w1.shape
    I = I2 // 2
    T = B * S // P
    G = T // 4
    ST = S // P
    NPART = 3
    KC = NPART * NPART * HD
    VC = 32
    OC = HD + 1
    REL = 2 * S
    RC = REL // P
    BW = S + (ST - 1) * P
    EPS = 1e-5
    SCALE = 1.0 / float(HD) ** 0.5
    HIGHEST = 3.0e38
    UNITS = H * B
    TILES = UNITS * ST
    BODY = 2 * B * ST

    qk_parts = nc.dram_tensor("qk_parts", (2, NPART, D, B * S), BF16).ap()
    qk_rows = nc.dram_tensor("qk_rows", (2, H, KC, B * S), BF16).ap()
    bias_dram = nc.dram_tensor("bias_rel", (H, REL), F32).ap()

    with ExitStack() as ctx:
        def sb(name, shape, dt=F32):
            return ctx.enter_context(nc.sbuf_tensor(name, shape, dt))

        def sem(name):
            return ctx.enter_context(nc.semaphore(name))

        ps = ctx.enter_context(nc.psum_tensor("ps", [P, 8, 512], F32))

        acc = sb("acc", [P, T, D])
        v_all = sb("v_all", [P, T, D])
        wg = sb("wg", [P, 2 * D])
        bg = sb("bg", [P, 2 * D])
        ident = sb("ident", [P, P])

        x_tok = x.rearrange("b s d -> (b s) d").rearrange("(t p) d -> p t d", p=P)
        out_tok = out.rearrange("b s d -> (b s) d").rearrange("(t p) d -> p t d", p=P)

        early = ctx.enter_context(ExitStack())

        def eb(name, shape, dt=F32):
            return early.enter_context(nc.sbuf_tensor(name, shape, dt))

        xh, xl = eb("xh", [P, T * P], F32R), eb("xl", [P, T * P], F32R)
        w1h, w1l = eb("w1h", [P, E, I2], F32R), eb("w1l", [P, E, I2], F32R)
        w2T = eb("w2T", [P, E, 2, D])
        comb = eb("comb", [P, T, E])
        gate_s = eb("gate_s", [P, 2, 512])
        y = eb("y", [P, 2, 2, 512])
        w1n = eb("w1n", [P, E, 4, D])
        w2n = eb("w2n", [P, E, I])
        wi = eb("wi", [P, 3 * D])
        flip = eb("flip", [P, P])
        xn = eb("xn", [P, 2, 4, D])
        xnT = eb("xnT", [P, 2, 512])
        xrev = eb("xrev", [P, 2, 512])
        resid = eb("resid", [P, 2, 512])
        parts = eb("parts", [P, 4, NPART, 512], BF16)
        par = eb("par", [P, 3, H * K])
        bt = eb("bt", [P, RC, H, K])
        bsum = eb("bsum", [P, RC, H])
        bsT = eb("bsT", [P, 2 * P])
        rel = eb("rel", [P, RC])
        stats = eb("stats", [P, T, 6])
        mv = eb("mv", [P, T, 2])
        std = eb("std", [P, T])
        rstd = eb("rstd", [P, T])
        eps = eb("eps", [P, 1])
        rtn = eb("rtn", [E, D])
        rT = eb("rT", [P, E])
        prio = eb("prio", [P, E])
        spare = y[:, :, :, :].rearrange("p a b c -> p (a b c)")
        small = spare[:, 0:7 * T * E].rearrange("p (n t e) -> p n t e", n=7, t=T)
        sm1 = spare[:, 7 * T * E:(7 * E + 6) * T].rearrange("p (n t) -> p n t", n=6)

        XG = G
        TG = T // XG
        s_x = [sem(f"x_loaded{i}") for i in range(XG)]
        s_win = sem("w_in_loaded")
        s_par = sem("bias_params_loaded")
        s_rt = sem("router_loaded")
        s_w1 = [sem(f"w1_loaded{i}") for i in range(4)]
        s_w2 = sem("w2_loaded")
        s_late = sem("gate_weights_loaded")
        s_eps = sem("eps_ready")
        s_id0 = sem("ident_zeroed")
        s_id = sem("ident_ready")
        s_fl = sem("flip_ready")
        s_xr = sem("xn_reversed")
        s_xrc = sem("xrev_copied")
        s_rel = sem("rel_ready")
        s_stats = sem("stats_done")
        s_mv = sem("mean_var_done")
        s_std = sem("std_done")
        s_rstd = sem("rstd_done")
        s_xn = sem("xn_done")
        s_xt = sem("xn_transposed")
        s_xte = sem("xnT_copied")
        s_qk = sem("qk_projected")
        s_p1 = sem("part1_done")
        s_r1 = sem("rest1_done")
        s_p2 = sem("part2_done")
        s_p3 = sem("part3_done")
        s_pst = [sem(f"parts_stored{i}") for i in range(4)]
        s_fill = sem("wide_filled")
        s_cp = sem("wide_copied")
        s_rtT = sem("router_transposed")
        s_rtc = sem("router_copied")
        s_log = sem("logits_done")
        s_dv = sem("router_step")
        s_re = sem("router_exp")
        s_d = sem("sharpness_ready")
        s_bq = sem("bias_square")
        s_bm = sem("bias_exponent")
        s_be = sem("bias_exp")
        s_ba = sem("bias_weighted")
        s_bs = sem("bias_summed")
        s_bT = sem("bias_transposed")
        s_bc = sem("bias_copied")
        s_bst = sem("bias_stored")

        s_gu = sem("gate_up_done")
        s_sg = sem("silu_done")
        s_y = sem("y_done")
        s_dn = sem("down_done")
        s_ac = sem("expert_added")
        s_row = sem("rows_stacked")
        s_xh = sem("x_high_done")
        s_xl = sem("x_rest_done")
        s_wl = sem("w1_rest_done")
        SQ = 4
        BQ = 4
        BIAS_STEP = 6

        def wait(eng, s, it, per, n):
            if isinstance(it, int):
                n, it = n + it * per, None
                if n <= 0:
                    return
            eng.wait_ge(s, n if it is None else it * per + n)

        def sweep(eng, times, body, lag, first, step):
            for k in range(first):
                step(0, k)
            with eng.Fori(0, times - 1) as it:
                for k in range(first, first + body):
                    step(it, k)
            for k in range(first, body + lag):
                step(times - 1, k)

        def tiles(it, k, s):
            n = (it + k // E) * 4 + s
            return slice(n, n + 1) if isinstance(it, int) else bass.ds(n, 1)

        def block_of(it, k):
            n = (it + k // E) * 512
            return slice(n, n + 512) if isinstance(it, int) else bass.ds(n, 512)

        def runs(it, k):
            return k >= 0 and (not isinstance(it, int) or it * E + k < G * E)

        def reversed_group(g):
            per = S // 512
            return g // per * per + per - 1 - g % per

        bt_flat = bt[:, :, :, :].rearrange("p c h k -> p c (h k)")
        with nc.Block() as block:
            @block.sync
            def _(sp):
                for i in range(XG):
                    sp.dma_start(acc[:, i * TG:(i + 1) * TG, :], x_tok[:, i * TG:(i + 1) * TG, :]).then_inc(s_x[i], 16)
                    if i == 0:
                        sp.dma_start(wi[:, :], w_in).then_inc(s_win, 16)
                for n, a in enumerate((amplitudes, sharpness, offsets)):
                    sp.dma_start(par[:, n, :], a.rearrange("h k -> (h k)").partition_broadcast(P)).then_inc(s_par, 16)
                sp.dma_start(rtn[:, :], router_w).then_inc(s_rt, 16)
                for i in range(4):
                    es = slice(i * E // 4, (i + 1) * E // 4)
                    sp.dma_start(w1n[:, es], w1[es].rearrange("e (j p) d -> p e j d", p=P)).then_inc(s_w1[i], 16)
                sp.dma_start(w2n[:, :, :], w2.rearrange("e h i -> h e i")).then_inc(s_w2, 16)
                sp.dma_start(wg[:, :], w_gate).then_inc(s_late, 16)
                sp.dma_start(bg[:, :], b_gate.partition_broadcast(P)).then_inc(s_late, 16)
                for j in range(2 * G):
                    g, w = j // 2, j % 2
                    if w:
                        g = reversed_group(g)
                    sp.wait_ge(s_p3, j + 1)
                    sp.wait_ge(s_p2, j + 1)
                    sp.dma_start(qk_parts[w, :, :, g * 512:(g + 1) * 512].rearrange("n d t -> d n t"),
                                 parts[:, j % 4, :, :]).then_inc(s_pst[j % 4], 16)
                for a in s_pst:
                    sp.wait_ge(a, 16 * 2 * G // 4)
                stacked = qk_rows.rearrange("w h (n m d) t -> w n m h d t", n=NPART, m=NPART)
                for n in range(NPART):
                    for m in range(NPART):
                        for w in range(2):
                            src = qk_parts[w, m if w else n].rearrange("(h d) t -> h d t", d=HD)
                            sp.dma_start(stacked[w, n, m], src).then_inc(s_row, 16)
                sp.wait_ge(s_bc, 1)
                for n in range(2):
                    sp.dma_start(bias_dram.rearrange("h (c r) -> c h r", r=P)[8 * n:8 * n + 8],
                                 bsT[:, n * P:(n + 1) * P]).then_inc(s_bst, 16)
                sp.wait_ge(s_row, 16 * 2 * NPART * NPART)
                sp.wait_ge(s_bst, 32)
                sp.wait_ge(s_late, 32)

            @block.gpsimd
            def _(pool):
                nc.gpsimd.memset(eps[:, :], EPS).then_inc(s_eps, 1)
                nc.gpsimd.memset(ident[:, :], 0.0).then_inc(s_id0, 1)
                pool.wait_ge(s_id0, 1)
                nc.gpsimd.affine_select(out=ident[:, :], in_=ident[:, :], compare_op=ALU.not_equal, fill=1.0,
                                        base=0, pattern=[[-1, P]], channel_multiplier=1).then_inc(s_id, 1)
                nc.gpsimd.memset(flip[:, :], 0.0).then_inc(s_fl, 1)
                pool.wait_ge(s_fl, 1)
                nc.gpsimd.affine_select(out=flip[:, :], in_=flip[:, :], compare_op=ALU.not_equal, fill=1.0,
                                        base=-(P - 1), pattern=[[1, P]], channel_multiplier=1).then_inc(s_fl, 1)
                nc.gpsimd.iota(rel[:, :], pattern=[[P, RC]], base=1 - S, channel_multiplier=1,
                               allow_small_or_imprecise_dtypes=True).then_inc(s_rel, 1)
                nc.gpsimd.iota(prio[:, :], pattern=[[-1, E]], base=E, channel_multiplier=0,
                               allow_small_or_imprecise_dtypes=True).then_inc(s_rel, 1)
                pool.wait_ge(s_d, 1)
                for c in range(RC):
                    pool.wait_ge(s_bq, c + 1)
                    nc.gpsimd.tensor_tensor(bt_flat[:, c, :], bt_flat[:, c, :], par[:, 1, :],
                                            ALU.mult).then_inc(s_bm, 1)
                for c in range(RC):
                    pool.wait_ge(s_be, c + 1)
                    nc.gpsimd.tensor_tensor(bt_flat[:, c, :], bt_flat[:, c, :], par[:, 0, :],
                                            ALU.mult).then_inc(s_ba, 1)

            @block.vector
            def _(dve):
                def statistics(i):
                    dve.wait_ge(s_x[i], 16)
                    for t in range(i * TG, (i + 1) * TG):
                        nc.vector.bn_stats(stats[:, t, :], acc[:, t, :]).then_inc(s_stats, 1)
                    for t in range(i * TG, (i + 1) * TG):
                        dve.wait_ge(s_stats, t + 1)
                        nc.vector.bn_aggr(mv[:, t, :], stats[:, t, :]).then_inc(s_mv, 1)

                def normalise(i):
                    dve.wait_ge(s_std, i + 1)
                    nc.vector.reciprocal(rstd[:, i * TG:(i + 1) * TG], std[:, i * TG:(i + 1) * TG]).then_inc(s_rstd, 1)
                    dve.wait_ge(s_rstd, i + 1)
                    if i >= 2:
                        dve.wait_ge(s_xt, i - 1)
                        dve.wait_ge(s_xr, i - 1)
                    for t in range(i * TG, (i + 1) * TG):
                        nc.vector.tensor_scalar(xn[:, i % 2, t % 4, :], acc[:, t, :], mv[:, t, 0:1], rstd[:, t:t + 1],
                                                ALU.subtract, ALU.mult).then_inc(s_xn, 1)

                statistics(0)
                statistics(1)
                normalise(0)
                statistics(2)
                normalise(1)

                dve.wait_ge(s_rtT, 1)
                nc.vector.tensor_copy(rT[:, :], ps[:, 6, 0:E]).then_inc(s_rtc, 1)

                def first_rest(j):
                    dve.wait_ge(s_p1, j + 1)
                    if j >= 2:
                        dve.wait_ge(s_p3, j - 1)
                    sc = SCALE if j % 2 == 0 else 1.0
                    nc.vector.scalar_tensor_tensor(out=resid[:, j % 2, :], in0=ps[:, 2 + j % 2, :], scalar=sc,
                                                   in1=parts[:, j % 4, 0, :], op0=ALU.mult,
                                                   op1=ALU.subtract).then_inc(s_r1, 1)

                def last_part(j):
                    dve.wait_ge(s_p2, j + 1)
                    nc.vector.tensor_tensor(parts[:, j % 4, 2, :], resid[:, j % 2, :], parts[:, j % 4, 1, :],
                                            ALU.subtract).then_inc(s_p3, 1)

                def x_rest(g):
                    dve.wait_ge(s_xh, g + 1)
                    cols = slice(g * 512, (g + 1) * 512)
                    nc.vector.tensor_tensor(xl[:, cols], ps[:, g % 2, :], xh[:, cols].bitcast(F32),
                                            ALU.subtract).then_inc(s_xl, 1)

                def w1_rest(e):
                    dve.wait_ge(s_cp, 2 * e + 2)
                    nc.vector.tensor_tensor(w1l[:, e, :], ps[:, 5, :], w1h[:, e, :].bitcast(F32),
                                            ALU.subtract).then_inc(s_wl, 1)

                for g in range(G):
                    if g + 2 < G:
                        normalise(g + 2)
                    x_rest(g)
                    first_rest(2 * g)
                    if g:
                        last_part(2 * g - 1)
                    first_rest(2 * g + 1)
                    last_part(2 * g)
                    if g + 3 < G:
                        statistics(g + 3)
                    if g == 0:
                        dve.wait_ge(s_par, 48)
                        nc.vector.scalar_tensor_tensor(out=par[:, 1, :], in0=par[:, 1, :], scalar=-1.0,
                                                       in1=par[:, 1, :], op0=ALU.mult, op1=ALU.max).then_inc(s_d, 1)
                    w1_rest(g)
                last_part(2 * G - 1)

                logits = ps[:, 6, 0:T * E].rearrange("p (t e) -> p t e", e=E)
                lg, pr, eq, sel1, rest, eq2, sel2 = (small[:, n] for n in range(7))
                mx, sm, rs, top, mxr, top2 = (sm1[:, n] for n in range(6))

                def bc(a):
                    return a.unsqueeze(2).to_broadcast([P, T, E])

                done = [0]

                def step(ins):
                    done[0] += 1
                    ins.then_inc(s_dv, 1)
                    dve.wait_ge(s_dv, done[0])

                pri = prio[:, :].unsqueeze(1).to_broadcast([P, T, E])
                dve.wait_ge(s_log, G)
                step(nc.vector.tensor_reduce(mx, logits, AX.X, ALU.max))
                step(nc.vector.tensor_tensor(lg, logits, bc(mx), ALU.subtract))
                dve.wait_ge(s_re, 1)
                step(nc.vector.tensor_reduce(sm, pr, AX.X, ALU.add))
                step(nc.vector.reciprocal(rs, sm))
                step(nc.vector.tensor_tensor(pr, pr, bc(rs), ALU.mult))
                step(nc.vector.tensor_reduce(mx, pr, AX.X, ALU.max))
                step(nc.vector.tensor_tensor(eq, pr, bc(mx), ALU.is_equal))
                step(nc.vector.tensor_tensor(eq, eq, pri, ALU.mult))
                step(nc.vector.tensor_reduce(top, eq, AX.X, ALU.max))
                step(nc.vector.tensor_tensor(sel1, eq, bc(top), ALU.is_equal))
                step(nc.vector.scalar_tensor_tensor(out=rest, in0=sel1, scalar=-2.0, in1=pr, op0=ALU.mult, op1=ALU.add))
                step(nc.vector.tensor_reduce(mxr, rest, AX.X, ALU.max))
                step(nc.vector.tensor_tensor(eq2, rest, bc(mxr), ALU.is_equal))
                step(nc.vector.tensor_tensor(eq2, eq2, pri, ALU.mult))
                step(nc.vector.tensor_reduce(top2, eq2, AX.X, ALU.max))
                step(nc.vector.tensor_tensor(sel2, eq2, bc(top2), ALU.is_equal))
                step(nc.vector.tensor_tensor(sel1, sel1, sel2, ALU.add))
                step(nc.vector.tensor_tensor(comb[:, :, :], sel1, pr, ALU.mult))

                def multiply(it, k):
                    for half in range(2):
                        n = 2 * k + half
                        wait(dve, s_sg, it, 2 * E, n + 1)
                        wait(dve, s_gu, it, 4 * E, 2 * n + 2)
                        wait(dve, s_dn, it, E, k - 1)
                        nc.vector.tensor_tensor(y[:, k % 2, half, :], ps[:, 2 * half + 1, :], gate_s[:, half, :],
                                                ALU.mult).then_inc(s_y, 1)

                def add(it, k):
                    wait(dve, s_dn, it, E, k + 1)
                    for s in range(4):
                        wait(dve, s_ac, it, 4 * E, 4 * (k - 1) + s + 1)
                        a = acc[:, tiles(it, k, s), :].rearrange("p a d -> p (a d)")
                        w = comb[:, tiles(it, k, s), k % E:k % E + 1].rearrange("p a d -> p (a d)")
                        nc.vector.scalar_tensor_tensor(out=a, in0=ps[:, 4 + k % 2, s * P:(s + 1) * P], scalar=w,
                                                       in1=a, op0=ALU.mult, op1=ALU.add).then_inc(s_ac, 1)

                def bias_sum(q):
                    dve.wait_ge(s_ba, RC)
                    c = slice(q * RC // BQ, (q + 1) * RC // BQ)
                    nc.vector.tensor_reduce(bsum[:, c, :], bt[:, c, :, :], AX.X, ALU.add).then_inc(s_bs, 1)

                def step(it, k):
                    if runs(it, k):
                        multiply(it, k)
                    if runs(it, k - 1):
                        add(it, k - 1)
                    if isinstance(it, int) and it:
                        if BIAS_STEP - BQ <= k - 1 < BIAS_STEP:
                            bias_sum(k - 1 - (BIAS_STEP - BQ))
                        if k == BIAS_STEP + 2:
                            dve.wait_ge(s_bT, 1)
                            nc.vector.tensor_copy(bsT[:, :], ps[:, 7, 0:2 * P]).then_inc(s_bc, 1)

                sweep(dve, G, E, 1, 3, step)

            @block.scalar
            def _(act):
                def deviation(i):
                    act.wait_ge(s_mv, (i + 1) * TG)
                    act.wait_ge(s_eps, 1)
                    nc.scalar.activation(std[:, i * TG:(i + 1) * TG], mv[:, i * TG:(i + 1) * TG, 1], ACT.Sqrt,
                                         bias=eps[:, 0:1], scale=1.0).then_inc(s_std, 1)

                def xnT_copy(g):
                    act.wait_ge(s_xt, g + 1)
                    if g >= 2:
                        act.wait_ge(s_qk, 2 * g - 3)
                        act.wait_ge(s_log, g - 1)
                    nc.scalar.copy(xnT[:, g % 2, :], ps[:, g % 2, :]).then_inc(s_xte, 1)
                    nc.scalar.copy(xh[:, g * 512:(g + 1) * 512], ps[:, g % 2, :]).then_inc(s_xh, 1)

                def xrev_copy(g):
                    act.wait_ge(s_xr, g + 1)
                    if g >= 2:
                        act.wait_ge(s_qk, 2 * g - 2)
                        act.wait_ge(s_fill, 2 * g - 3)
                    nc.scalar.copy(xrev[:, g % 2, :], ps[:, 7, :]).then_inc(s_xrc, 1)

                def first_part(j):
                    act.wait_ge(s_qk, j + 1)
                    if j >= 4:
                        act.wait_ge(s_pst[j % 4], 16 * (j // 4))
                    sc = SCALE if j % 2 == 0 else 1.0
                    nc.scalar.mul(parts[:, j % 4, 0, :], ps[:, 2 + j % 2, :], sc).then_inc(s_p1, 1)

                def second_part(j):
                    act.wait_ge(s_r1, j + 1)
                    nc.scalar.copy(parts[:, j % 4, 1, :], resid[:, j % 2, :]).then_inc(s_p2, 1)

                def wide_copy(n):
                    act.wait_ge(s_fill, n + 1)
                    src = ps[:, 4 + n % 2, :]
                    if n >= 2 * G:
                        m = n - 2 * G
                        nc.scalar.copy(w2T[:, 2 * m:2 * m + 2, :, :].rearrange("p e i d -> p (e i d)"),
                                       src).then_inc(s_cp, 1)
                    elif n % 2:
                        nc.scalar.copy(w1h[:, n // 2, :], src).then_inc(s_cp, 1)
                    else:
                        k = 4 * reversed_group(n // 2)
                        nc.scalar.copy(v_all[:, k:k + 4, :].rearrange("p t d -> p (t d)"), src).then_inc(s_cp, 1)

                def bias_square(c):
                    nc.scalar.activation(bt_flat[:, c, :], par[:, 2, :], ACT.Square,
                                         bias=rel[:, c:c + 1]).then_inc(s_bq, 1)

                def bias_exp(c):
                    act.wait_ge(s_bm, c + 1)
                    nc.scalar.activation(bt_flat[:, c, :], bt_flat[:, c, :], ACT.Exp, scale=-1.0).then_inc(s_be, 1)

                for i in range(3):
                    deviation(i)
                xnT_copy(0)
                xrev_copy(0)
                for g in range(G):
                    if g + 1 < G:
                        xnT_copy(g + 1)
                        xrev_copy(g + 1)
                    first_part(2 * g)
                    if g:
                        second_part(2 * g - 1)
                    first_part(2 * g + 1)
                    second_part(2 * g)
                    wide_copy(2 * g)
                    wide_copy(2 * g + 1)
                    for n in range(4):
                        if g == 0 and n == 0:
                            act.wait_ge(s_par, 48)
                            act.wait_ge(s_rel, 2)
                        if g < SQ:
                            bias_square(RC // SQ * g + n)
                        else:
                            bias_exp(RC // SQ * (g - SQ) + n)
                        if n == 3 and g + 3 < G:
                            deviation(g + 3)
                second_part(2 * G - 1)
                for n in range(2 * G, 2 * G + E // 2):
                    wide_copy(n)
                act.wait_ge(s_dv, 2)
                nc.scalar.activation(small[:, 1], small[:, 0], ACT.Exp).then_inc(s_re, 1)

                def step(it, k):
                    for half in range(2):
                        n = 2 * k + half
                        wait(act, s_gu, it, 4 * E, 2 * n + 1)
                        wait(act, s_y, it, 2 * E, n - 1)
                        nc.scalar.activation(gate_s[:, half, :], ps[:, 2 * half, :], ACT.Silu).then_inc(s_sg, 1)

                sweep(act, G, E, 0, 2, step)

            @block.tensor
            def _(pe):
                pe.wait_ge(s_id, 1)
                pe.wait_ge(s_rt, 16)
                nc.tensor.transpose(ps[:, 6, 0:E], rtn[:, :], ident[0:E, 0:E]).then_inc(s_rtT, 1)

                def turn_xn(g):
                    pe.wait_ge(s_xn, 4 * g + 4)
                    if g >= 2:
                        pe.wait_ge(s_xte, g - 1)
                        pe.wait_ge(s_xh, g - 1)
                        pe.wait_ge(s_xl, g - 1)
                    for t in range(4):
                        mm = nc.tensor.transpose(ps[:, g % 2, t * P:(t + 1) * P], xn[:, g % 2, t, :], ident[:, :])
                    mm.then_inc(s_xt, 1)

                def turn_reversed(g):
                    if g >= 1:
                        pe.wait_ge(s_xrc, g)
                    for t in range(4):
                        mm = nc.tensor.transpose(ps[:, 7, (3 - t) * P:(4 - t) * P], xn[:, g % 2, t, :], flip[:, :])
                    mm.then_inc(s_xr, 1)

                def project(j):
                    g, w = j // 2, j % 2
                    pe.wait_ge(s_xrc if w else s_xte, g + 1)
                    if j >= 2:
                        pe.wait_ge(s_p1, j - 1)
                        pe.wait_ge(s_r1, j - 1)
                    col = 2 * D if w == 0 else 0
                    tokens = xrev[:, g % 2, :] if w else xnT[:, g % 2, :]
                    nc.tensor.matmul(ps[:, 2 + j % 2, :], wi[:, col:col + D], tokens,
                                     start=True, stop=True).then_inc(s_qk, 1)

                def route(g):
                    for t in range(4):
                        k = 4 * g + t
                        mm = nc.tensor.matmul(ps[:, 6, k * E:(k + 1) * E], xnT[:, g % 2, t * P:(t + 1) * P], rT[:, :],
                                              start=True, stop=True)
                    mm.then_inc(s_log, 1)

                def wide(n):
                    if n >= 2:
                        pe.wait_ge(s_cp, n - 1)
                    if n % 2 and n >= 3:
                        pe.wait_ge(s_wl, min(n // 2, E))
                    for t in range(4):
                        dst = ps[:, 4 + n % 2, t * P:(t + 1) * P]
                        if n >= 2 * G:
                            e = 2 * (n - 2 * G) + t // 2
                            mm = nc.tensor.transpose(dst, w2n[:, e, t % 2 * P:(t % 2 + 1) * P], ident[:, :])
                        elif n % 2:
                            mm = nc.tensor.transpose(dst, w1n[:, n // 2, t, :], ident[:, :])
                        else:
                            mm = nc.tensor.matmul(dst, xrev[:, n // 2 % 2, t * P:(t + 1) * P], wi[:, D:2 * D],
                                                  start=True, stop=True)
                    mm.then_inc(s_fill, 1)

                turn_xn(0)
                pe.wait_ge(s_fl, 2)
                turn_reversed(0)
                pe.wait_ge(s_win, 16)
                pe.wait_ge(s_rtc, 1)
                for g in range(G):
                    if g + 1 < G:
                        turn_xn(g + 1)
                        turn_reversed(g + 1)
                    project(2 * g)
                    project(2 * g + 1)
                    wide(2 * g)
                    route(g)
                    if g % (E // 4) == 0:
                        pe.wait_ge(s_w1[g * 4 // E], 16)
                    wide(2 * g + 1)
                pe.wait_ge(s_w2, 16)
                for n in range(2 * G, 2 * G + E // 2):
                    wide(n)
                pe.wait_ge(s_xl, G)
                pe.wait_ge(s_xh, G)
                pe.wait_ge(s_p1, 2 * G)
                pe.wait_ge(s_r1, 2 * G)
                pe.wait_ge(s_cp, 2 * G + E // 2)
                pe.wait_ge(s_xrc, G)

                def gate_up(it, k):
                    e = k % E
                    for half in range(2):
                        n = 2 * k + half
                        wait(pe, s_y, it, 2 * E, n - 1)
                        for u in range(2):
                            cols = slice(u * I + half * P, u * I + half * P + P)
                            dst, blk = ps[:, 2 * half + u, :], block_of(it, k)
                            nc.tensor.matmul(dst, w1h[:, e, cols], xh[:, blk], start=True, stop=False)
                            nc.tensor.matmul(dst, w1h[:, e, cols], xl[:, blk], start=False, stop=False)
                            nc.tensor.matmul(dst, w1l[:, e, cols], xh[:, blk],
                                             start=False, stop=True).then_inc(s_gu, 1)

                def down(it, k):
                    wait(pe, s_y, it, 2 * E, 2 * k + 2)
                    wait(pe, s_ac, it, 4 * E, 4 * (k - 1))
                    for s in range(4):
                        for half in range(2):
                            mm = nc.tensor.matmul(ps[:, 4 + k % 2, s * P:(s + 1) * P],
                                                  y[:, k % 2, half, s * P:(s + 1) * P], w2T[:, k % E, half, :],
                                                  start=(half == 0), stop=(half == 1))
                    mm.then_inc(s_dn, 1)

                def turn_bias():
                    pe.wait_ge(s_bs, BQ)
                    bflat = bsum[:, :, :].rearrange("p c h -> p (c h)")
                    for n in range(2):
                        mm = nc.tensor.transpose(ps[:, 7, n * P:(n + 1) * P], bflat[:, n * P:(n + 1) * P], ident[:, :])
                    mm.then_inc(s_bT, 1)

                def step(it, k):
                    if runs(it, k):
                        gate_up(it, k)
                    if runs(it, k - 1):
                        down(it, k - 1)
                    if isinstance(it, int) and it and k == BIAS_STEP + 1:
                        turn_bias()

                sweep(pe, G, E, 1, 3, step)

        early.close()

        ST_LAG, PV_LAG = 15, 19
        MAX_AT = ST + 2
        assert 2 * ST + MAX_AT == ST - 1 + PV_LAG
        KM = P - NPART
        PAD = P // 2
        AG, AD = 656, 944
        WG = AG // 2
        WD, WP = AD - AG, S - AD
        RING = 4
        st = sb("st", [P, RING, AG])
        z = sb("z", [P, RING, AD])
        pT = sb("pT", [P, RING, S])
        biased_s = sb("biased_s", [P, 2, S])
        bias = sb("bias", [P, 2, BW])
        qs = sb("qs", [P, 4, S], BF16)
        ks = sb("ks", [P, 4, S], BF16)
        ones = sb("ones", [NPART, S], BF16)
        vu = sb("vu", [P, 2, ST, VC])
        negmax = sb("negmax", [P, 2, ST])
        mres = sb("mres", [P, ST])
        m3 = sb("m3", [P, NPART, ST], BF16)
        mT = sb("mT", [NPART * ST, 2, P], BF16)
        ident_b = sb("ident_b", [P, P], BF16)
        oT = sb("oT", [P, H * B, 2 * P])
        ones_p = sb("ones_p", [P, ST * HD])
        s_vz = sem("constants_ready")
        s_z = sem("pad_zeroed")
        s_one = sem("ones_loaded")
        s_ql = [sem(f"qk_loaded{i}") for i in range(4)]
        s_mr = [sem(f"max_rows_loaded{i}") for i in range(4)]
        s_bl = [sem(f"bias_loaded{i}") for i in range(2)]
        s_vc = sem("v_copied")
        s_s = sem("scores_done")
        s_m = sem("max_done")
        s_mp = sem("max_split_step")
        s_mt = sem("max_transposed")
        s_mc = sem("max_copied")
        s_tg = sem("st_for_gpsimd")
        s_moved = sem("st_moved")
        s_td = sem("st_for_vector_and_biased")
        s_ga = sem("bias_added_by_gpsimd")
        s_da = sem("bias_added_by_vector")
        s_ep = sem("exp_from_psum_done")
        s_e = sem("exp_done")
        s_pv = sem("pv_piece_done")
        s_ev = sem("out_kept")

        def within(it, k):
            return k >= 0 and (not isinstance(it, int) or it * BODY + k < TILES)

        LOADS = 2
        U = BODY // ST
        HT = B * ST
        FIRST = 4 * ST

        def bias_there(eng, it, k):
            if k % HT == 0:
                hh = k // HT
                wait(eng, s_bl[hh % 2], it, 16, 16 * (hh // 2 + 1))

        with nc.Block() as block:
            @block.sync
            def _(sp):
                def load_unit(it, u):
                    wait(sp, s_td, it, BODY, ST * (u - 3))
                    h = it * 2 + u // B
                    b = u % B
                    col = slice(b * S, (b + 1) * S)
                    for w, dst in enumerate((qs, ks)):
                        src = qk_rows[w, h, :, col] if isinstance(it, int) else \
                            qk_rows[w, bass.ds(h, 1), :, col].rearrange("a r t -> (a r) t")
                        sp.dma_start(dst[0:KC, u % 4, :], src).then_inc(s_ql[u % 4], 16)

                def load_max(it, u):
                    wait(sp, s_mc, it, U, u + 1)
                    for n in range(NPART):
                        sp.dma_start(qs[KM + n:KM + n + 1, u % 4, :].rearrange("a (t q) -> a t q", q=P),
                                     mT[n * ST:(n + 1) * ST, u % 2, :]).then_inc(s_mr[u % 4], 16)

                def load_bias(it, hh):
                    wait(sp, s_e, it, BODY, HT * (hh - 1))
                    h = it * 2 + hh
                    row = bias_dram[h, :] if isinstance(it, int) else bias_dram[bass.ds(h, 1), :]
                    src = bass.AP(row.tensor, row.offset, [[1, P], [1, BW]])
                    sp.dma_start(bias[:, hh % 2, :], src).then_inc(s_bl[hh % 2], 16)

                load_bias(0, 0)
                sp.wait_ge(s_z, 2)
                load_unit(0, 0)
                sp.wait_ge(s_z, 4)
                load_unit(0, 1)
                sp.wait_ge(s_z, 8)
                sp.wait_ge(s_vz, 1)
                for i in range(4):
                    sp.dma_start(ks[KM:P, i, :], ones[:, :]).then_inc(s_one, 16)
                load_bias(0, 1)

                def step(it, u):
                    if not isinstance(it, int) or it * U + u + 2 < H * B:
                        load_unit(it, u + 2)
                    load_max(it, u)
                    hh = (u + 3) // B
                    if u % B == 1 and u > B and (not isinstance(it, int) or it * 2 + hh < H):
                        load_bias(it, hh)

                sweep(sp, H * B // U, U, 0, 5, step)

            @block.gpsimd
            def _(pool):
                nc.gpsimd.memset(ones[:, :], 1.0).then_inc(s_vz, 1)
                nc.gpsimd.memset(vu[:, :, :, :], 0.0).then_inc(s_vz, 1)
                nc.gpsimd.tensor_copy(ident_b[:, :], ident[:, :]).then_inc(s_vz, 1)
                nc.gpsimd.memset(ones_p[:, :], 1.0).then_inc(s_vz, 1)
                pool.wait_ge(s_vz, 4)
                nc.gpsimd.memset(vu[:, :, :, HD:HD + 1], 1.0).then_inc(s_vz, 1)
                pool.wait_ge(s_vz, 5)

                def copy_v(it, u):
                    wait(pool, s_pv, it, BODY, ST * (u - 1))
                    h = it * 2 + u // B
                    b = u % B
                    cols = slice(h * HD, (h + 1) * HD) if isinstance(it, int) else bass.ds(h * HD, HD)
                    v = v_all[:, b * ST:(b + 1) * ST, cols]
                    nc.gpsimd.tensor_tensor(vu[:, u % 2, :, 0:HD], v,
                                            ones_p[:, :].rearrange("p (t c) -> p t c", c=HD), ALU.mult).then_inc(s_vc, 1)

                def split_max(it, u):
                    nm = negmax[:, u % 2, :]
                    wait(pool, s_m, it, BODY, ST * (u + 1))
                    wait(pool, s_mt, it, U, u)
                    nc.gpsimd.tensor_tensor(m3[:, 0, :], nm, ones_p[:, 0:ST], ALU.mult).then_inc(s_mp, 1)
                    wait(pool, s_mp, it, 4 * U, 4 * u + 1)
                    nc.gpsimd.tensor_tensor(mres[:, :], nm, m3[:, 0, :], ALU.subtract).then_inc(s_mp, 1)
                    wait(pool, s_mp, it, 4 * U, 4 * u + 2)
                    nc.gpsimd.tensor_tensor(m3[:, 1, :], mres[:, :], ones_p[:, 0:ST], ALU.mult).then_inc(s_mp, 1)
                    wait(pool, s_mp, it, 4 * U, 4 * u + 3)
                    nc.gpsimd.tensor_tensor(m3[:, 2, :], mres[:, :], m3[:, 1, :], ALU.subtract).then_inc(s_mp, 1)

                def add(it, k):
                    bias_there(pool, it, k)
                    off = (k % ST) * P
                    wait(pool, s_moved, it, BODY, k + 1)
                    nc.gpsimd.tensor_tensor(z[:, k % RING, 0:AG], st[:, k % RING, :],
                                            bias[:, (k // HT) % 2, off:off + AG], ALU.add).then_inc(s_ga, 1)

                def step(it, k):
                    if k % ST == 0 and within(it, k - ST):
                        split_max(it, k // ST - 1)
                    if within(it, k - ST_LAG):
                        add(it, k - ST_LAG)
                    if k % ST == 4 and within(it, k - 4 - ST):
                        copy_v(it, k // ST - 1)

                sweep(pool, TILES // BODY, BODY, ST_LAG, FIRST, step)

            @block.tensor
            def _(pe):
                def scores(it, k):
                    u = k // ST
                    if k % ST == 0:
                        wait(pe, s_ql[u % 4], it, 16 * LOADS * U // 4, 16 * LOADS * (u // 4 + 1))
                    wait(pe, s_m, it, BODY, k - 1)
                    for n in range(2):
                        mm = nc.tensor.matmul(ps[:, 2 * (k % 2) + n, :],
                                              qs[0:KM, u % 4, (k % ST) * P:(k % ST + 1) * P],
                                              ks[0:KM, u % 4, n * 512:(n + 1) * 512], start=True, stop=True)
                    mm.then_inc(s_s, 1)

                def scores_t(it, k):
                    u = k // ST
                    if k % ST == 0:
                        wait(pe, s_mr[u % 4], it, 16 * NPART * U // 4, 16 * NPART * (u // 4 + 1))
                    if isinstance(it, int) and it * BODY + k == 0:
                        pe.wait_ge(s_one, 64)
                    keys = ks[:, u % 4, (k % ST) * P:(k % ST + 1) * P]
                    wait(pe, s_moved, it, BODY, k)
                    for n in range(2):
                        mm = nc.tensor.matmul(ps[:, 4 + n, 0:WG], keys, qs[:, u % 4, n * WG:(n + 1) * WG],
                                              start=True, stop=True)
                    mm.then_inc(s_tg, 1)

                def last_scores_t(it, k):
                    u = k // ST
                    keys = ks[:, u % 4, (k % ST) * P:(k % ST + 1) * P]
                    off = (k % ST) * P
                    bias_there(pe, it, k)
                    wait(pe, s_da, it, BODY, k)
                    nc.tensor.matmul(ps[:, 6, WD:WD + WP], keys, qs[:, u % 4, AD:S], start=True, stop=False)
                    nc.tensor.matmul(ps[:, 6, WD:WD + WP], ident[:, :], bias[:, (k // HT) % 2, off + AD:off + S],
                                     start=False, stop=True)
                    nc.tensor.matmul(ps[:, 6, 0:WD], keys, qs[:, u % 4, AG:AD],
                                     start=True, stop=True).then_inc(s_td, 1)

                def weigh(it, k):
                    u, kt = k // ST, k % ST
                    if kt == 0:
                        wait(pe, s_vc, it, U, u + 1)
                        wait(pe, s_ev, it, U, u)
                        if within(it, k + ST):
                            wait(pe, s_mc, it, U, u + 2)
                    wait(pe, s_e, it, BODY, k + 1)
                    for j in range(4):
                        mm = nc.tensor.matmul(ps[32 * j:32 * j + 32, 7, 0:256], vu[:, u % 2, kt, :],
                                              pT[:, k % RING, j * 256:(j + 1) * 256],
                                              start=(kt == 0), stop=(kt == ST - 1), tile_position=(0, 32 * j))
                    mm.then_inc(s_pv, 1)

                def turn_max(it, u):
                    wait(pe, s_mp, it, 4 * U, 4 * u + 4)
                    wait(pe, s_mc, it, U, u)
                    nc.tensor.matmul(ps[0:NPART * ST, 7, 256:256 + P], m3[:, :, :].rearrange("p n t -> p (n t)"),
                                     ident_b[:, :], start=True, stop=True).then_inc(s_mt, 1)

                def step(it, k):
                    if within(it, k):
                        scores(it, k)
                    if within(it, k - ST_LAG):
                        scores_t(it, k - ST_LAG)
                    if within(it, k - PV_LAG):
                        weigh(it, k - PV_LAG)
                    if within(it, k - ST_LAG):
                        last_scores_t(it, k - ST_LAG)
                    if k % ST == MAX_AT % ST and within(it, k - MAX_AT):
                        if isinstance(it, int) and it * BODY + k == MAX_AT:
                            pe.wait_ge(s_vz, 5)
                        turn_max(it, (k - MAX_AT) // ST)

                sweep(pe, TILES // BODY, BODY, PV_LAG, FIRST, step)

            @block.vector
            def _(dve):
                for i in range(4):
                    nc.vector.memset(qs[PAD:P, i, :], 0.0).then_inc(s_z, 1)
                    nc.vector.memset(ks[PAD:P, i, :], 0.0).then_inc(s_z, 1)

                def may_add(it, k):
                    bias_there(dve, it, k)
                    if k % ST == 0:
                        wait(dve, s_mp, it, 4 * U, 4 * (k // ST - 1))
                    wait(dve, s_s, it, BODY, k + 1)

                def add_max(it, k):
                    off = (k % ST) * P
                    nc.vector.tensor_tensor_reduce(
                        biased_s[:, k % 2, :], ps[:, 2 * (k % 2):2 * (k % 2) + 2, :].rearrange("p a b -> p (a b)"),
                        bias[:, (k // HT) % 2, off:off + S], -1.0, HIGHEST, ALU.add, ALU.min,
                        negmax[:, (k // ST) % 2, k % ST:k % ST + 1]).then_inc(s_m, 1)

                def add(it, k):
                    wait(dve, s_ep, it, BODY, k + 1)
                    off = (k % ST) * P
                    nc.vector.tensor_tensor(z[:, k % RING, AG:AD], ps[:, 6, 0:WD],
                                            bias[:, (k // HT) % 2, off + AG:off + AD], ALU.add).then_inc(s_da, 1)

                def step(it, k):
                    if within(it, k):
                        may_add(it, k)
                    if within(it, k - ST_LAG - 1):
                        add(it, k - ST_LAG - 1)
                    if within(it, k):
                        add_max(it, k)

                sweep(dve, TILES // BODY, BODY, ST_LAG + 1, FIRST, step)

            @block.scalar
            def _(act):
                def move(it, k):
                    wait(act, s_tg, it, BODY, k + 1)
                    nc.scalar.copy(st[:, k % RING, :].rearrange("p (n q) -> p n q", n=2),
                                   ps[:, 4:6, 0:WG]).then_inc(s_moved, 1)

                def exp_psum(it, k):
                    wait(act, s_td, it, BODY, k + 1)
                    nc.scalar.activation(pT[:, k % RING, AD:S], ps[:, 6, WD:WD + WP], ACT.Exp).then_inc(s_ep, 1)

                def expo(it, k):
                    wait(act, s_ga, it, BODY, k + 1)
                    if not within(it, k + 1):
                        wait(act, s_da, it, BODY, k + 1)
                    nc.scalar.activation(pT[:, k % RING, 0:AD], z[:, k % RING, :], ACT.Exp).then_inc(s_e, 1)

                def keep_out(it, u):
                    wait(act, s_pv, it, BODY, ST * (u + 1))
                    dst = oT[:, it * U + u, :] if isinstance(it, int) else \
                        oT[:, bass.ds(it * U + u, 1), :].rearrange("p a q -> p (a q)")
                    nc.scalar.copy(dst, ps[:, 7, 0:256]).then_inc(s_ev, 1)

                def copy_max(it, u):
                    wait(act, s_mt, it, U, u + 1)
                    v = u - 2
                    if v >= 0 or not isinstance(it, int):
                        wait(act, s_mr[v % 4], it, 16 * NPART * U // 4, 16 * NPART * (v // 4 + 1))
                    nc.scalar.copy(mT[:, u % 2, :], ps[0:NPART * ST, 7, 256:256 + P]).then_inc(s_mc, 1)

                def step(it, k):
                    if within(it, k - ST_LAG):
                        move(it, k - ST_LAG)
                        exp_psum(it, k - ST_LAG)
                    if k % ST == MAX_AT % ST:
                        u = (k - MAX_AT) // ST
                        if within(it, k - MAX_AT):
                            copy_max(it, u)
                        if u >= 2:
                            keep_out(it, u - 2)
                    if within(it, k - ST_LAG - 2):
                        expo(it, k - ST_LAG - 2)

                sweep(act, TILES // BODY, BODY, PV_LAG + 1, FIRST, step)

        arena = pT[:, :, :].rearrange("p a b -> p (a b)")
        attn = arena[:, 0:1024].rearrange("p (a t d) -> p a t d", a=2, t=4)
        attnT = arena[:, 1024:2048].rearrange("p (a q) -> p a q", a=2)
        rsum = arena[:, 2048:2048 + 2 * 4 * H].rearrange("p (a h j) -> p a h j", a=2, j=4)
        free = z[:, :, :].rearrange("p a b -> p (a b)")
        gated = free[:, 0:3 * 512].rearrange("p (a t c) -> p a t c", a=3, t=2)
        sig = free[:, 3 * 512:3 * 768].rearrange("p (a t c) -> p a t c", a=3, t=2)
        s_ot = sem("out_transposed")
        s_rc = sem("sums_inverted")
        s_an = sem("attn_normalised")
        s_at = sem("attn_transposed")
        s_atc = sem("attnT_copied")
        s_gt = sem("gate_projected")
        s_gb = sem("gate_biased")
        s_si = sem("sigmoid_done")
        s_ml = sem("gated_done")
        s_fi = sem("result_done")
        s_out = sem("result_stored")
        NP2 = T // 2

        def group_tiles(g, lo, hi):
            first = ST * (g // 2) + g % 2
            return slice(first + 2 * lo, first + 2 * hi - 1, 2)

        with nc.Block() as block:
            @block.vector
            def _(dve):
                def norm(g, half):
                    o = ps[:, 2 * half:2 * half + 2, :].rearrange("p k (h j c) -> p (k h) j c", h=4, j=4)
                    hs = slice(half * H // 2, (half + 1) * H // 2)
                    dve.wait_ge(s_ot, 2 * g + half + 1)
                    if g >= 2:
                        dve.wait_ge(s_at, g - 1)
                    nc.vector.reciprocal(rsum[:, g % 2, hs], o[:, :, :, HD]).then_inc(s_rc, 1)
                    dve.wait_ge(s_rc, 2 * g + half + 1)
                    nc.vector.tensor_tensor(
                        attn[:, g % 2, :, half * D // 2:(half + 1) * D // 2].rearrange("p j (h c) -> p h j c", c=HD),
                        o[:, :, :, 0:HD], rsum[:, g % 2, hs].unsqueeze(3).to_broadcast([P, H // 2, 4, HD]),
                        ALU.mult).then_inc(s_an, 1)

                def biased(n):
                    dve.wait_ge(s_gt, n + 1)
                    if n >= 3:
                        dve.wait_ge(s_ml, n - 2)
                    nc.vector.tensor_tensor(gated[:, n % 3], ps[:, 4 + n % 2, :].rearrange("p (t c) -> p t c", t=2),
                                            bg[:, :].unsqueeze(1).to_broadcast([P, 2, 2 * D]),
                                            ALU.add).then_inc(s_gb, 1)

                def final(n):
                    dve.wait_ge(s_ml, n + 1)
                    a = acc[:, group_tiles(n // 2, 2 * (n % 2), 2 * (n % 2) + 2), :]
                    nc.vector.tensor_tensor(a, a, sig[:, n % 3], ALU.add).then_inc(s_fi, 1)

                for n in range(3):
                    norm(n // 2, n % 2)
                for n in range(NP2 + 2):
                    if n + 3 < 2 * G:
                        norm((n + 3) // 2, (n + 3) % 2)
                    if n < NP2:
                        biased(n)
                    if n >= 2:
                        final(n - 2)

            @block.gpsimd
            def _(pool):
                for n in range(NP2):
                    pool.wait_ge(s_si, n + 1)
                    nc.gpsimd.tensor_tensor(sig[:, n % 3], gated[:, n % 3, :, 0:D], sig[:, n % 3],
                                            ALU.mult).then_inc(s_ml, 1)

            @block.scalar
            def _(act):
                def copy_t(g):
                    act.wait_ge(s_at, g + 1)
                    if g >= 2:
                        act.wait_ge(s_gt, 2 * g - 2)
                    nc.scalar.copy(attnT[:, g % 2, :], ps[:, 6 + g % 2, :]).then_inc(s_atc, 1)

                copy_t(0)
                for n in range(NP2):
                    if n % 2 == 0 and n // 2 + 1 < G:
                        copy_t(n // 2 + 1)
                    act.wait_ge(s_gb, n + 1)
                    if n >= 3:
                        act.wait_ge(s_fi, n - 2)
                    nc.scalar.activation(sig[:, n % 3], gated[:, n % 3, :, D:2 * D], ACT.Sigmoid).then_inc(s_si, 1)

            @block.tensor
            def _(pe):
                def turn_out(g, half):
                    b, s = g // 2, g % 2
                    if g:
                        pe.wait_ge(s_an, 2 * g - 1 + half)
                    for h in range(half * H // 2, (half + 1) * H // 2):
                        mm = nc.tensor.transpose(ps[:, h // 4, (h % 4) * P:(h % 4 + 1) * P],
                                                 oT[:, h * B + b, s * P:(s + 1) * P], ident[:, :])
                    mm.then_inc(s_ot, 1)

                def turn_attn(g):
                    pe.wait_ge(s_an, 2 * g + 2)
                    if g >= 2:
                        pe.wait_ge(s_atc, g - 1)
                    for t in range(4):
                        mm = nc.tensor.transpose(ps[:, 6 + g % 2, t * P:(t + 1) * P], attn[:, g % 2, t, :], ident[:, :])
                    mm.then_inc(s_at, 1)

                for g in range(2):
                    turn_out(g, 0)
                    turn_out(g, 1)
                turn_attn(0)
                for n in range(NP2):
                    g = n // 2
                    if n % 2 == 0:
                        pe.wait_ge(s_atc, g + 1)
                    if n >= 2:
                        pe.wait_ge(s_gb, n - 1)
                    for t in range(2):
                        k = 2 * (n % 2) + t
                        mm = nc.tensor.matmul(ps[:, 4 + n % 2, t * 2 * D:(t + 1) * 2 * D],
                                              attnT[:, g % 2, k * P:(k + 1) * P], wg[:, :], start=True, stop=True)
                    mm.then_inc(s_gt, 1)
                    if n % 2 == 0 and g + 1 < G:
                        turn_attn(g + 1)
                    if g + 2 < G:
                        turn_out(g + 2, n % 2)

            @block.sync
            def _(sp):
                for g in range(G):
                    sp.wait_ge(s_fi, 2 * g + 2)
                    t = group_tiles(g, 0, 4)
                    sp.dma_start(out_tok[:, t, :], acc[:, t, :]).then_inc(s_out, 16)
                sp.wait_ge(s_out, 16 * G)


_INS = ['L0_attn_x', 'L0_attn_w_in', 'L0_attn_w_gate', 'L0_attn_b_gate', 'L0_attn_amplitudes', 'L0_attn_sharpness',
        'L0_attn_offsets', 'L0_ffn_w1', 'L0_ffn_w2', 'L0_ffn_router_w']
_OUTS = [((4, 1024, 128), 'float32')]


def kernel(**inputs):
    import numpy as _np
    import concourse.bacc as _bacc
    from concourse import mybir as _mybir
    from concourse.bass_utils import run_bass_kernel_spmd as _run

    nc = _bacc.Bacc("TRN2", target_bir_lowering=False, num_devices=1)
    arrays, args = {}, []
    for name in _INS:
        a = _np.ascontiguousarray(inputs[name])
        arrays[f"in_{name}_dram"] = a
        args.append(nc.dram_tensor(f"in_{name}_dram", a.shape, _mybir.dt.from_np(a.dtype), kind="ExternalInput").ap())
    for i, (shape, dtype) in enumerate(_OUTS):
        dt = _mybir.dt.from_np(_np.dtype(dtype))
        args.append(nc.dram_tensor(f"out_{i}_dram", shape, dt, kind="ExternalOutput").ap())
    fused_layer(nc, *args)
    r = _run(nc, [arrays], core_ids=[0])
    return r.results[0]["out_0_dram"]
```
